# Optimizing a Trainium2 kernel written in Bass

```python
import numpy as np
import jax
import jax.numpy as jnp

def _softmax(x, axis=-1):
    return jax.nn.softmax(x, axis=axis)

def _gelu(x):
    return jax.nn.gelu(x, approximate=True)

def _silu(x):
    return jax.nn.silu(x)

def _sigmoid(x):
    return jax.nn.sigmoid(x)

def _layernorm(x, axis=-1, eps=1e-05):
    m = jnp.mean(x, axis=axis, keepdims=True)
    v = jnp.var(x, axis=axis, keepdims=True)
    return (x - m) / jnp.sqrt(v + eps)

def _scatter_add(tgt, idx, src, axis=0):
    return tgt.at[idx].add(src)

def _segment_sum(src, seg, n):
    return jax.ops.segment_sum(src, seg, n)
kernel_name = 'mk_adj_ffn_d1_adj_r2_82391d'

def setup_inputs(seed: int=0):
    np.random.seed(seed)
    _w = jnp.asarray

    def _rec_inputs():
        import jax
        import jax.numpy as jnp
        _gk = jax.random.key(seed)
        x = -0.0002928 + 1 * jax.random.normal(jax.random.fold_in(_gk, 1), (3327, 256), jnp.float32)
        _a = jax.random.bernoulli(jax.random.fold_in(_gk, 2), 0.00120228, (3327, 3327))
        _a = jnp.logical_or(_a, jnp.swapaxes(_a, -1, -2))
        _a = jnp.logical_or(_a, jnp.eye(3327, dtype=bool))
        _af = _a.astype(jnp.float32)
        _af = _af * jax.random.uniform(jax.random.fold_in(_gk, 3), (3327, 3327), jnp.float32, 0.05, 1)
        adj = _af
        return (x, adj)
    x, adj = _rec_inputs()

    def _L0_gnn_setup():
        import jax, jax.numpy as jnp
        import numpy as np
        N = 4096
        F_IN = 256
        F_OUT = 256
        key = jax.random.key(seed)
        k1, k2, k3, k4 = jax.random.split(key, 4)
        stdv = 1.0 / np.sqrt(F_OUT)
        inp = jax.random.normal(k1, (N, F_IN), dtype=jnp.float32)
        adj = jax.random.uniform(k2, (N, N), dtype=jnp.float32)
        weight = jax.random.uniform(k3, (F_IN, F_OUT), minval=-stdv, maxval=stdv, dtype=jnp.float32)
        bias = jax.random.uniform(k4, (F_OUT,), minval=-stdv, maxval=stdv, dtype=jnp.float32)
        return {'inp': inp, 'adj': adj, 'weight': weight, 'bias': bias}
    _L0_gnn_all = _L0_gnn_setup()
    _L0_gnn_in = {k: v for k, v in _L0_gnn_all.items() if k in ('weight', 'bias')}
    del _L0_gnn_all

    def _L0_ffn_setup():
        import jax, jax.numpy as jnp
        import numpy as np
        DIM = 256
        HID = 768
        N_EXPERTS = 8
        TOP_K = 2
        SHARED_HID = HID * 2
        B, S = (4, 1024)

        def _swiglu(x, w1, w3, w2):
            return jax.nn.silu(x @ w1.T) * (x @ w3.T) @ w2.T
        key = jax.random.key(seed)
        ks = jax.random.split(key, 8)
        sc_d = 1.0 / np.sqrt(DIM)
        sc_h = 1.0 / np.sqrt(HID)
        sc_sh = 1.0 / np.sqrt(SHARED_HID)
        return {'x': jax.random.normal(ks[0], (B, S, DIM), jnp.float32), 'gate_w': jax.random.normal(ks[1], (N_EXPERTS, DIM), jnp.float32) * sc_d, 'w1': jax.random.normal(ks[2], (N_EXPERTS, HID, DIM), jnp.float32) * sc_d, 'w3': jax.random.normal(ks[3], (N_EXPERTS, HID, DIM), jnp.float32) * sc_d, 'w2': jax.random.normal(ks[4], (N_EXPERTS, DIM, HID), jnp.float32) * sc_h, 'sw1': jax.random.normal(ks[5], (SHARED_HID, DIM), jnp.float32) * sc_d, 'sw3': jax.random.normal(ks[6], (SHARED_HID, DIM), jnp.float32) * sc_d, 'sw2': jax.random.normal(ks[7], (DIM, SHARED_HID), jnp.float32) * sc_sh}
    _L0_ffn_all = _L0_ffn_setup()
    _L0_ffn_in = {k: v for k, v in _L0_ffn_all.items() if k in ('gate_w', 'w1', 'w3', 'w2', 'sw1', 'sw3', 'sw2')}
    del _L0_ffn_all
    return {'x': x, 'adj': adj, 'L0_gnn_weight': _L0_gnn_in['weight'], 'L0_gnn_bias': _L0_gnn_in['bias'], 'L0_ffn_gate_w': _L0_ffn_in['gate_w'], 'L0_ffn_w1': _L0_ffn_in['w1'], 'L0_ffn_w3': _L0_ffn_in['w3'], 'L0_ffn_w2': _L0_ffn_in['w2'], 'L0_ffn_sw1': _L0_ffn_in['sw1'], 'L0_ffn_sw3': _L0_ffn_in['sw3'], 'L0_ffn_sw2': _L0_ffn_in['sw2']}

def reference(x, adj, L0_gnn_weight, L0_gnn_bias, L0_ffn_gate_w, L0_ffn_w1, L0_ffn_w3, L0_ffn_w2, L0_ffn_sw1, L0_ffn_sw3, L0_ffn_sw2):
    import jax
    import jax.numpy as jnp

    def _L0_gnn_ref(inp, adj, weight, bias):
        import jax, jax.numpy as jnp
        import numpy as np
        N = 4096
        F_IN = 256
        F_OUT = 256
        support = jnp.matmul(inp, weight)
        return jnp.matmul(adj, support) + bias

    def _L0_ffn_ref(x, gate_w, w1, w3, w2, sw1, sw3, sw2):
        import jax, jax.numpy as jnp
        import numpy as np
        DIM = 256
        HID = 768
        N_EXPERTS = 8
        TOP_K = 2
        SHARED_HID = HID * 2
        B, S = (4, 1024)

        def _swiglu(x, w1, w3, w2):
            return jax.nn.silu(x @ w1.T) * (x @ w3.T) @ w2.T
        b, s, d = x.shape
        t = b * s
        xf = x.reshape(t, d)
        logits = xf.astype(jnp.float32) @ gate_w.astype(jnp.float32).T
        scores = jax.nn.softmax(logits, axis=-1)
        topk_w, topk_i = jax.lax.top_k(scores, TOP_K)
        e = gate_w.shape[0]
        comb = jnp.zeros((t, e), jnp.float32).at[jnp.arange(t)[:, None], topk_i].add(topk_w)
        y = jnp.zeros((t, d), x.dtype)
        for i in range(e):
            ye = _swiglu(xf, w1[i], w3[i], w2[i]).astype(x.dtype)
            y = y + comb[:, i:i + 1].astype(x.dtype) * ye
        y = y.reshape(b, s, d)
        shared = _swiglu(xf, sw1, sw3, sw2).reshape(b, s, d).astype(x.dtype)
        return y + shared
    x = x + _L0_gnn_ref(_layernorm(x, axis=-1), adj, L0_gnn_weight, L0_gnn_bias)
    x = x + _L0_ffn_ref(_layernorm(x, axis=-1)[None], L0_ffn_gate_w, L0_ffn_w1, L0_ffn_w3, L0_ffn_w2, L0_ffn_sw1, L0_ffn_sw3, L0_ffn_sw2)[0]
    return x

_drawn_inputs = setup_inputs


def setup_inputs(seed=0):
    import zlib

    import numpy as np

    out = dict(_drawn_inputs(seed))
    spreads = {}
    factors = {}
    for name, (base, spread) in spreads.items():
        noise = np.random.default_rng([zlib.crc32(name.encode()), seed]).standard_normal(out[name].shape)
        drawn = base * np.exp(spread * noise) if base else spread * noise
        out[name] = jnp.asarray(drawn.astype(out[name].dtype))
    for name, factor in factors.items():
        out[name] = (out[name] * factor).astype(out[name].dtype)
    return out
```

```python
from contextlib import ExitStack

import numpy as np

import concourse.bass as bass
from concourse import mybir

F32 = mybir.dt.float32
F32R = mybir.dt.float32r
I32 = mybir.dt.int32
U32 = mybir.dt.uint32
ALU = mybir.AluOpType
ACT = mybir.ActivationFunctionType
AX_X = mybir.AxisListType.X

P = 128
N = 3327
D = 256
DC = D // P
E = 8
HID = 768
HC = HID // P
HALF = HID // 2
TILES = -(-N // P)
NP = TILES * P
HALF_J = TILES // 2
UA = TILES
UB = 2 * TILES
SLOTS = (2 * NP) // P + E - 1
UNITS = UB + SLOTS
ROW = D + 4
ID_COL, W_COL = D, D + 1
PART = DC * HID
WCOLS = 3 * PART
RING = 4
EPS = 1e-5
IDENT, TRI, ONES, IOTA8, IOTA_S = 0, P, 2 * P, 3 * P, 3 * P + E
CST = IOTA_S + SLOTS


def at_least(eng, sem, value):
    if isinstance(value, int) and value <= 0:
        return
    eng.wait_ge(sem, value)


def build(nc, x, adj, w_gnn, bias, gate, weights, cst, out):
    xn_dram = nc.dram_tensor("xn_dram", [NP, ROW], F32, kind="Internal").ap()
    sorted_dram = nc.dram_tensor("sorted_dram", [SLOTS * P, ROW], F32, kind="Internal").ap()

    place = [-(-nc.sbuf_base // 32) * 32]

    def sb(name, cols, dt=F32, parts=P):
        t = nc.alloc_sbuf_tensor_at(name, [parts, cols], dt, offset=place[0])
        place[0] += -(-cols * 4 // 32) * 32
        return t

    ctx = ExitStack()
    with ctx:
        x_all = sb("x_all", TILES * D)
        xn2_all = sb("xn2_all", TILES * ROW)
        raw_w = sb("raw_w", WCOLS)
        consts = sb("consts", CST)
        small = sb("small", 64)
        zrow = sb("zrow", ROW)
        gate_raw = sb("gate_raw", DC * E)
        gate_h = sb("gate_h", DC * E, F32R)
        gate_l = sb("gate_l", DC * E, F32R)
        w_start = place[0]
        W = nc.alloc_sbuf_tensor_at("W", [P, 2 * 2 * WCOLS], F32R, offset=w_start)
        first_layer = w_start + 2 * WCOLS * 4
        place[0] = first_layer
        s_hl = sb("s_hl", TILES * 2 * D, F32R)
        adj_raw = [sb(f"adj_raw{h}", HALF_J * P) for h in range(2)]
        adj_h, adj_l = [], []
        for h in range(2):
            support_only = place[0]
            adj_h.append(sb(f"adj_h{h}", HALF_J * P, F32R))
            adj_l.append(sb(f"adj_l{h}", HALF_J * P, F32R))
        bias_sb = sb("bias_sb", D)
        assert place[0] <= nc.sbuf_usable_end, (place[0], nc.sbuf_usable_end)
        place[0] = support_only
        w_gnn_raw = sb("w_gnn_raw", DC * D)
        w_gnn_h = sb("w_gnn_h", DC * D, F32R)
        w_gnn_l = sb("w_gnn_l", DC * D, F32R)
        xn = sb("xn", D)
        xnT_h = sb("xnT_h", D, F32R)
        xnT_l = sb("xnT_l", D, F32R)
        assert place[0] <= support_only + 2 * HALF_J * P * 4
        place[0] = first_layer + 2 * WCOLS * 4
        xt = sb("xt", ROW)
        xT_h = sb("xT_h", D, F32R)
        xT_l = sb("xT_l", D, F32R)
        sil = [sb(f"sil{h}", HALF) for h in range(2)]
        g = [sb(f"g{h}", HALF) for h in range(2)]
        gT_h = [sb(f"gT_h{h}", HALF, F32R) for h in range(2)]
        gT_l = [sb(f"gT_l{h}", HALF, F32R) for h in range(2)]
        y_ring = sb("y_ring", RING * D)
        id_ring = sb("id_ring", RING, I32)
        meta_id = sb("meta_id", RING, I32)
        meta_w = sb("meta_w", RING)
        logit = sb("logit", E)
        m8 = sb("m8", E)
        i8 = sb("i8", E, U32)
        i2f = sb("i2f", 2)
        m8_all = sb("m8_all", TILES * E)
        oh1 = sb("oh1", TILES * E)
        oh2 = sb("oh2", TILES * E)
        chosen = sb("chosen", TILES * E)
        before = sb("before", (TILES + 1) * E)
        pos_e = sb("pos_e", TILES * E)
        tmp1 = sb("tmp1", TILES * E)
        tmp2 = sb("tmp2", TILES * E)
        esum = sb("esum", TILES)
        w2 = sb("w2", TILES)
        pos1f = sb("pos1f", TILES)
        pos2f = sb("pos2f", TILES)
        pos1 = sb("pos1", TILES, I32)
        pos2 = sb("pos2", TILES, I32)
        n_i = sb("n_i", E, I32)
        n_t = sb("n_t", E, I32)
        tiles_f = sb("tiles_f", E)
        ones8 = sb("ones8", E)
        end_f = sb("end_f", E)
        start_f = sb("start_f", E)
        slot8a = sb("slot8a", SLOTS * E, parts=1)
        slot8b = sb("slot8b", SLOTS * E, parts=1)
        e_of = sb("e_of", SLOTS + 1, parts=1)
        end_of = sb("end_of", SLOTS, parts=1)
        next_of = sb("next_of", SLOTS, parts=1)
        first_of = sb("first_of", SLOTS, parts=1)
        ones_s = sb("ones_s", SLOTS, parts=1)
        run_of = sb("run_of", SLOTS + 1, parts=1)
        flag_of = sb("flag_of", SLOTS, parts=1)
        run_i = sb("run_i", SLOTS + 1, I32, parts=1)
        par_i = sb("par_i", SLOTS + 1, I32, parts=1)
        flag_i = sb("flag_i", SLOTS, I32, parts=1)
        fetch_i = [sb(f"fetch_i{b}", SLOTS, I32, parts=1) for b in range(2)]
        next_i = sb("next_i", SLOTS, I32, parts=1)
        e0_i = sb("e0_i", 1, I32, parts=1)
        assert place[0] <= nc.sbuf_usable_end
        bank = [ctx.enter_context(nc.psum_tensor(f"bank{b}", [P, 512], F32)) for b in range(8)]

        st, mv, sd, rs, eps = small[:, 0:6], small[:, 6:8], small[:, 8:9], small[:, 9:10], small[:, 10:11]
        st2, mv2, sd2, rs2 = small[:, 16:22], small[:, 22:24], small[:, 24:25], small[:, 25:26]
        ident = consts[:, IDENT:IDENT + P]
        tri = consts[:, TRI:TRI + P]
        ones_pp = consts[:, ONES:ONES + P]
        iota8 = consts[:, IOTA8:IOTA8 + E]

        def sem(name):
            return ctx.enter_context(nc.semaphore(name))

        s_x = [sem("s_x_in0"), sem("s_x_in1")]; s_small_in = sem("s_small_in"); s_cst = sem("s_cst"); s_bias = sem("s_bias"); s_gate_in = sem("s_gate_in")
        s_adj = [sem("s_adj0"), sem("s_adj1")]
        s_raw_w = [sem(f"s_raw_w{i}") for i in range(3)]
        s_prefill = sem("s_prefill"); s_trash = sem("s_trash"); s_xn_out = sem("s_xn_out"); s_xt = sem("s_xt")
        s_sort1 = sem("s_sort1"); s_sort2 = sem("s_sort2"); s_out = sem("s_out"); s_add = sem("s_add")
        s_passed = sem("s_passed"); s_eps = sem("s_eps"); s_zero = sem("s_zero"); s_zid = sem("s_zid"); s_wg = sem("s_wg"); s_gate = sem("s_gate"); s_ids = sem("s_ids"); s_init = sem("s_init")
        s_bn = sem("s_bn"); s_mv = sem("s_mv"); s_sd = sem("s_sd"); s_rs = sem("s_rs"); s_xn = sem("s_xn")
        s_xnT = sem("s_xnT"); s_xnh = sem("s_xnh"); s_xnl = sem("s_xnl"); s_smm = sem("s_smm"); s_sh = sem("s_sh"); s_sl = sem("s_sl")
        s_biased = sem("s_biased")
        s_ah = sem("s_ah"); s_al = sem("s_al"); s_half = [sem("s_half0"), sem("s_half1")]; s_acc = s_half[1]
        s_t1 = sem("s_t1"); s_x1 = sem("s_x1"); s_bn2 = sem("s_bn2"); s_mv2 = sem("s_mv2"); s_sd2 = sem("s_sd2"); s_rs2 = sem("s_rs2"); s_xn2 = sem("s_xn2")
        s_wh = sem("s_wh"); s_wl = sem("s_wl")
        s_xT = sem("s_xT"); s_xTh = sem("s_xTh"); s_xTl = sem("s_xTl"); s_meta = sem("s_meta")
        s_up = [sem("s_up0"), sem("s_up1")]; s_sil = [sem("s_sil0"), sem("s_sil1")]; s_g = [sem("s_g0"), sem("s_g1")]
        s_gT = [sem("s_gT0"), sem("s_gT1")]; s_gTh = [sem("s_gTh0"), sem("s_gTh1")]; s_gTl = [sem("s_gTl0"), sem("s_gTl1")]
        s_down = sem("s_down"); s_y = sem("s_y")
        s_m8 = sem("s_m8"); s_i8 = sem("s_i8"); s_i2f = sem("s_i2f"); s_oh = sem("s_oh"); s_chosen = sem("s_chosen"); s_before = sem("s_before")
        s_rank = sem("s_rank"); s_rank_read = sem("s_rank_read"); s_dlog = sem("s_dlog"); s_exp = sem("s_exp")
        s_r = sem("s_r"); s_pos = sem("s_pos"); s_w1 = sem("s_w1"); s_w2 = sem("s_w2"); s_tables = sem("s_tables")

        block = ctx.enter_context(nc.Block())

        def own_wait(eng, sem, value):
            at_least(eng, sem, value)
            if not isinstance(value, int):
                eng.sem_inc(s_passed, 1)

        def rows(t):
            return bass.ds(t * P, P)

        def xtile(t):
            return x_all[:, bass.ds(t * D, D)]

        def load_expert(eng, e, n):
            for part in range(3):
                at_least(eng, s_wl, 3 * (n - 1) + part + 1)
                eng.dma_start(raw_w[:, part * PART:(part + 1) * PART],
                              weights[rows(e * 3 + part), :]).then_inc(s_raw_w[part], 16)

        @block.sync
        def _(sp):
            sp.dma_start(x_all[:, 0:2 * D], x[:, 0:2 * D]).then_inc(s_x[0], 16)
            sp.dma_start(w_gnn_raw[:, :], w_gnn).then_inc(s_small_in, 16)
            sp.dma_start(consts[:, :], cst).then_inc(s_cst, 16)
            sp.dma_start(x_all[:, 2 * D:], x[:, 2 * D:]).then_inc(s_x[1], 16)
            sp.dma_start(bias_sb[:, :], bias).then_inc(s_bias, 16)
            sp.dma_start(gate_raw[:, :], gate).then_inc(s_gate_in, 16)

            def adj_load(t, h):
                at_least(sp, s_al, 2 * t - 1 + h)
                sp.dma_start(adj_raw[h][:, :], adj[rows(t), h * HALF_J * P:(h + 1) * HALF_J * P]).then_inc(s_adj[h], 16)

            def xn_store(t):
                sp.wait_ge(s_xn2, t + 1)
                sp.dma_start(xn_dram[rows(t), :], xn2_all[:, bass.ds(t * ROW, ROW)]).then_inc(s_xn_out, 16)

            for t in range(2):
                for h in range(2):
                    adj_load(t, h)
                if t == 0:
                    load_expert(sp, 0, 0)
            sp.wait_ge(s_ids, TILES)
            sp.wait_ge(s_init, 1)
            with sp.Fori(2, TILES) as t:
                adj_load(t, 0)
                adj_load(t, 1)
                xn_store(t - 2)
            xn_store(TILES - 2)
            xn_store(TILES - 1)
            load_expert(sp, 1, 1)

            def unit_load(u, source, tile):
                at_least(sp, s_xT, u)
                at_least(sp, s_meta, u)
                sp.dma_start(xt[:, :], source[rows(tile), :]).then_inc(s_xt, 16)

            sp.wait_ge(s_xn_out, 16 * TILES)
            sp.wait_ge(s_acc, TILES)
            sp.wait_ge(s_al, 2 * TILES)
            unit_load(0, xn_dram, 0)
            with sp.Fori(1, UA) as u:
                unit_load(u, xn_dram, u)
            with sp.Fori(UA, UB) as u:
                unit_load(u, xn_dram, u - UA)
            sp.wait_ge(s_tables, 1)
            load_expert(sp, sp.value_load(e0_i[0:1, 0:1], min_val=0, max_val=E - 1) + 2, 2)
            sp.wait_ge(s_sort1, 16 * TILES)
            sp.wait_ge(s_sort2, 16 * TILES)
            unit_load(UB, sorted_dram, 0)
            unit_load(UB + 1, sorted_dram, 1)

            def fetch(s):
                flag = sp.value_load(flag_i[0:1, bass.ds(s, 1)], min_val=0, max_val=1)
                with sp.If(flag > 0):
                    e = sp.value_load(next_i[0:1, bass.ds(s, 1)], min_val=0, max_val=E - 1)
                    run1 = sp.value_load(run_i[0:1, bass.ds(s + 1, 1)], min_val=1, max_val=E)
                    load_expert(sp, e + 2, run1 + 2)

            with sp.Fori(0, SLOTS - 2) as s:
                unit_load(UB + 2 + s, sorted_dram, s + 2)
                fetch(s)
            for s in range(SLOTS - 2, SLOTS):
                fetch(s)

        @block.gpsimd
        def _(pool):
            pool.memset(zrow[:, :], 0.0).then_inc(s_zero, 1)
            pool.memset(xn2_all[:, :], 0.0).then_inc(s_init, 1)
            pool.wait_ge(s_zero, 1)
            pool.iota(zrow[:, ID_COL:ID_COL + 1].bitcast(I32), [[0, 1]], base=NP, channel_multiplier=1).then_inc(s_zid, 1)
            pool.wait_ge(s_zid, 1)
            pool.wait_ge(s_init, 1)
            for t in range(TILES):
                pool.iota(xn2_all[:, t * ROW + ID_COL:t * ROW + ID_COL + 1].bitcast(I32), [[0, 1]], base=t * P,
                          channel_multiplier=1).then_inc(s_ids, 1)
            pool.wait_ge(s_bias, 16)
            with pool.Fori(0, TILES) as t:
                own_wait(pool, s_xn, t + 1)
                pool.tensor_tensor(xtile(t), xtile(t), bias_sb[:, :], ALU.add).then_inc(s_biased, 1)
            pool.dma_start(out[rows(TILES), :], zrow[:, 0:D]).then_inc(s_trash, 16)
            with pool.Fori(0, SLOTS) as s:
                pool.dma_start(sorted_dram[rows(s), :], zrow[:, :]).then_inc(s_prefill, 16)

            def split_expert(n, buffer):
                for part in range(3):
                    high = W[:, buffer * (2 * WCOLS) + part * PART:][:, :PART]
                    low = W[:, buffer * (2 * WCOLS) + WCOLS + part * PART:][:, :PART]
                    raw = raw_w[:, part * PART:(part + 1) * PART]
                    own_wait(pool, s_raw_w[part], 16 * (n + 1))
                    pool.tensor_scalar(high, raw, 1.0, 1.0, ALU.mult, ALU.mult).then_inc(s_wh, 1)
                    pool.wait_ge(s_wh, 3 * n + part + 1)
                    pool.tensor_tensor(low, raw, high.bitcast(F32), ALU.subtract).then_inc(s_wl, 1)

            split_expert(0, 0)
            pool.wait_ge(s_acc, TILES)
            split_expert(1, 1)
            pool.wait_ge(s_prefill, 16 * SLOTS)
            for which, (pos, ready, done) in enumerate(((pos1, s_w1, s_sort1), (pos2, s_w2, s_sort2))):
                pool.wait_ge(s_pos, 2)
                pool.wait_ge(ready, 1)
                for t in range(TILES):
                    pool.indirect_dma_start(sorted_dram[:, :], bass.IndirectOffsetOnAxis(ap=pos[:, t:t + 1], axis=0),
                                            xn2_all[:, t * ROW:(t + 1) * ROW], None).then_inc(done, 16)
            pool.wait_ge(s_down, UA)
            split_expert(2, 0)
            pool.wait_ge(s_y, UB + 1)
            pool.dma_start(out[0:NP, :].rearrange("(t p) d -> p t d", p=P),
                           x_all[:, :].rearrange("p (t d) -> p t d", d=D)).then_inc(s_out, 16)
            pool.wait_ge(s_out, 16)
            pool.wait_ge(s_trash, 16)

            def routed_unit(s, slot):
                for buffer in range(2):
                    flag = pool.value_load(fetch_i[buffer][0:1, bass.ds(s, 1)], min_val=0, max_val=1)
                    with pool.If(flag > 0):
                        run1 = pool.value_load(run_i[0:1, bass.ds(s + 1, 1)], min_val=1, max_val=E)
                        own_wait(pool, s_down, s + UB)
                        split_expert(run1 + 2, buffer)
                own_wait(pool, s_y, s + (UB + 2))
                if not isinstance(s, int) or s > 0:
                    own_wait(pool, s_add, s * 16)
                pool.indirect_dma_start(out[:, :], bass.IndirectOffsetOnAxis(ap=id_ring[:, slot:slot + 1], axis=0),
                                        y_ring[:, slot * D:(slot + 1) * D], None, compute_op=ALU.add).then_inc(s_add, 16)

            for s in range(RING):
                routed_unit(s, s)
            with pool.Fori(1, SLOTS // RING) as q:
                for slot in range(RING):
                    routed_unit(q * RING + slot, slot)
            for s in range(SLOTS // RING * RING, SLOTS):
                routed_unit(s, s % RING)
            pool.wait_ge(s_add, 16 * SLOTS)

        @block.scalar
        def _(act):
            def support(t):
                if not isinstance(t, int) or t >= 2:
                    own_wait(act, s_smm, t - 1)
                    act.activation(s_hl[:, bass.ds((t - 2) * (2 * D), D)], bank[2][:, 0:D], ACT.Copy).then_inc(s_sh, 1)
                if not isinstance(t, int) or 1 <= t <= TILES:
                    act.wait_ge(s_xnT, t)
                    act.activation(xnT_h[:, :], bank[0][:, 0:D], ACT.Copy).then_inc(s_xnh, 1)
                if not isinstance(t, int) or t < TILES:
                    act.wait_ge(s_mv, t + 1)
                    if isinstance(t, int) and t == 0:
                        act.wait_ge(s_eps, 1)
                    act.activation(sd, mv[:, 1:2], ACT.Sqrt, bias=eps).then_inc(s_sd, 1)

            support(0)
            support(1)
            with act.Fori(2, TILES) as t:
                support(t)
            support(TILES)
            support(TILES + 1)

            def neighbours(t):
                for h in range(2):
                    act.wait_ge(s_adj[h], 16 * t + 16)
                    at_least(act, s_half[h], t)
                    if isinstance(t, int) and t == 0 and h == 1:
                        act.wait_ge(s_sl, TILES)
                    act.activation(adj_h[h][:, :], adj_raw[h][:, :], ACT.Copy).then_inc(s_ah, 1)
                std(t - 1)

            def std(t):
                if isinstance(t, int) and t < 0:
                    return
                act.wait_ge(s_mv2, t + 1)
                act.activation(sd2, mv2[:, 1:2], ACT.Sqrt, bias=eps).then_inc(s_sd2, 1)

            neighbours(0)
            with act.Fori(1, TILES) as t:
                neighbours(t)
            std(TILES - 1)

            def high_gT(u, h):
                act.wait_ge(s_gT[h], u + 1)
                act.activation(gT_h[h][:, :], bank[4 + h][:, 0:HALF], ACT.Copy).then_inc(s_gTh[h], 1)

            def high_xT(u):
                act.wait_ge(s_xT, u + 1)
                at_least(act, s_up[1], u)
                act.activation(xT_h[:, :], bank[6][:, 0:D], ACT.Copy).then_inc(s_xTh, 1)

            def silu(u, h):
                act.wait_ge(s_up[h], u + 1)
                at_least(act, s_g[h], u)
                act.activation(sil[h][:, :], bank[2 * h][:, 0:HALF], ACT.Silu).then_inc(s_sil[h], 1)

            def unit(u, last=False):
                first = isinstance(u, int) and u == 0
                if not first:
                    high_gT(u - 1, 0)
                silu(u, 0)
                if not first:
                    high_gT(u - 1, 1)
                if not last:
                    high_xT(u + 1)
                silu(u, 1)

            act.wait_ge(s_xn2, TILES)
            high_xT(0)
            unit(0)
            with act.Fori(1, UA + 2) as u:
                unit(u)
            act.wait_ge(s_dlog, 1)
            act.activation(tmp2[:, :], tmp1[:, :], ACT.Exp).then_inc(s_exp, 1)
            with act.Fori(UA + 2, UNITS - 1) as u:
                unit(u)
            unit(UNITS - 1, last=True)
            high_gT(UNITS - 1, 0)
            high_gT(UNITS - 1, 1)

        @block.vector
        def _(dve):
            dve.memset(eps, EPS).then_inc(s_eps, 1)
            dve.wait_ge(s_small_in, 16)
            dve.tensor_copy(w_gnn_h[:, :], w_gnn_raw[:, :]).then_inc(s_wg, 1)
            dve.wait_ge(s_wg, 1)
            dve.tensor_tensor(w_gnn_l[:, :], w_gnn_raw[:, :], w_gnn_h[:, :].bitcast(F32), ALU.subtract).then_inc(s_wg, 1)

            def support(t):
                whole = not isinstance(t, int)
                if whole or t < TILES:
                    if not whole and t < 4:
                        dve.wait_ge(s_x[min(t // 2, 1)], 16)
                    if whole or t > 0:
                        own_wait(dve, s_mv, t)
                    dve.bn_stats(st, xtile(t)).then_inc(s_bn, 1)
                if whole or t >= 2:
                    dve.wait_ge(s_sh, t - 1)
                    dve.tensor_tensor(s_hl[:, bass.ds((t - 2) * (2 * D) + D, D)], bank[2][:, 0:D],
                                      s_hl[:, bass.ds((t - 2) * (2 * D), D)].bitcast(F32), ALU.subtract).then_inc(s_sl, 1)
                if whole or t < TILES:
                    at_least(dve, s_xn, t)
                    own_wait(dve, s_bn, t + 1)
                    dve.bn_aggr(mv, st).then_inc(s_mv, 1)
                if whole or 1 <= t <= TILES:
                    dve.wait_ge(s_xnh, t)
                    dve.tensor_tensor(xnT_l[:, :], bank[0][:, 0:D], xnT_h[:, :].bitcast(F32), ALU.subtract).then_inc(s_xnl, 1)
                if whole or t < TILES:
                    dve.wait_ge(s_sd, t + 1)
                    dve.reciprocal(rs, sd).then_inc(s_rs, 1)
                    dve.wait_ge(s_rs, t + 1)
                    at_least(dve, s_xnT, t)
                    dve.tensor_scalar(xn[:, :], xtile(t), mv[:, 0:1], rs, ALU.subtract, ALU.mult).then_inc(s_xn, 1)

            for t in range(4):
                support(t)
            with dve.Fori(4, TILES) as t:
                support(t)
            support(TILES)
            support(TILES + 1)
            dve.wait_ge(s_gate_in, 16)
            dve.tensor_copy(gate_h[:, :], gate_raw[:, :]).then_inc(s_gate, 1)
            dve.wait_ge(s_gate, 1)
            dve.tensor_tensor(gate_l[:, :], gate_raw[:, :], gate_h[:, :].bitcast(F32), ALU.subtract).then_inc(s_gate, 1)

            def low_adj(t, h):
                dve.wait_ge(s_ah, 2 * t + h + 1)
                dve.tensor_tensor(adj_l[h][:, :], adj_raw[h][:, :], adj_h[h][:, :].bitcast(F32), ALU.subtract).then_inc(s_al, 1)

            def residual(t, acc):
                dve.wait_ge(s_acc, t + 1)
                dve.wait_ge(s_biased, t + 1)
                dve.tensor_tensor(xtile(t), acc[:, 0:D], xtile(t), ALU.add).then_inc(s_t1, 1)
                dve.wait_ge(s_t1, t + 1)
                dve.tensor_tensor(xtile(t), acc[:, D:2 * D], xtile(t), ALU.add).then_inc(s_x1, 1)
                at_least(dve, s_mv2, t)
                own_wait(dve, s_x1, t + 1)
                dve.bn_stats(st2, xtile(t)).then_inc(s_bn2, 1)

            def norm_mean(t):
                at_least(dve, s_xn2, t)
                own_wait(dve, s_bn2, t + 1)
                dve.bn_aggr(mv2, st2).then_inc(s_mv2, 1)

            def norm(t):
                dve.wait_ge(s_sd2, t + 1)
                dve.reciprocal(rs2, sd2).then_inc(s_rs2, 1)
                dve.wait_ge(s_rs2, t + 1)
                if isinstance(t, int) and t == 0:
                    dve.wait_ge(s_init, 1)
                dve.tensor_scalar(xn2_all[:, bass.ds(t * ROW, D)], xtile(t), mv2[:, 0:1], rs2,
                                  ALU.subtract, ALU.mult).then_inc(s_xn2, 1)

            def row_block(t, acc_before):
                low_adj(t, 0)
                low_adj(t, 1)
                if isinstance(t, int) and t == 0:
                    return
                residual(t - 1, acc_before)
                norm_mean(t - 1)
                norm(t - 1)

            row_block(0, None)
            row_block(1, bank[4])
            with dve.Fori(1, TILES // 2) as pair:
                row_block(2 * pair, bank[5])
                row_block(2 * pair + 1, bank[4])
            residual(TILES - 1, bank[5])
            norm_mean(TILES - 1)
            norm(TILES - 1)

            def low_gT(u, h):
                dve.wait_ge(s_gTh[h], u + 1)
                dve.tensor_tensor(gT_l[h][:, :], bank[4 + h][:, 0:HALF], gT_h[h][:, :].bitcast(F32), ALU.subtract).then_inc(s_gTl[h], 1)

            def product(u, h):
                dve.wait_ge(s_sil[h], u + 1)
                at_least(dve, s_gT[h], u)
                dve.tensor_tensor(g[h][:, :], bank[2 * h + 1][:, 0:HALF], sil[h][:, :], ALU.mult).then_inc(s_g[h], 1)

            def low_xT(u):
                own_wait(dve, s_xTh, u + 1)
                dve.tensor_copy(meta_id[:, bass.ds(u % RING, 1)], xt[:, ID_COL:ID_COL + 1].bitcast(I32))
                dve.tensor_copy(meta_w[:, bass.ds(u % RING, 1)], xt[:, W_COL:W_COL + 1]).then_inc(s_meta, 1)
                dve.tensor_tensor(xT_l[:, :], bank[6][:, 0:D], xT_h[:, :].bitcast(F32), ALU.subtract).then_inc(s_xTl, 1)

            def shared_y(u, tile):
                dve.wait_ge(s_down, u + 1)
                return dve.tensor_tensor(xtile(tile), bank[7][:, 0:D], xtile(tile), ALU.add)

            def routed_y(u):
                s = u - UB
                r = s % RING
                at_least(dve, s_add, 16 * (s - RING + 1))
                dve.wait_ge(s_meta, u + 1)
                own_wait(dve, s_down, u + 1)
                dve.tensor_copy(id_ring[:, bass.ds(r, 1)], meta_id[:, bass.ds(u % RING, 1)])
                dve.tensor_scalar(y_ring[:, bass.ds(r * D, D)], bank[7][:, 0:D], meta_w[:, bass.ds(u % RING, 1)],
                                  None, ALU.mult).then_inc(s_y, 1)

            def tile8(buf, t):
                return buf[:, bass.ds(t * E, E)]

            def count(t):
                dve.wait_ge(s_oh, 2 * t + 2)
                dve.tensor_tensor(tile8(chosen, t), tile8(oh1, t), tile8(oh2, t), ALU.add).then_inc(s_chosen, 1)
                dve.wait_ge(s_chosen, t + 1)
                dve.wait_ge(s_before, t + 1)
                dve.tensor_tensor(tile8(before, t + 1), tile8(before, t), tile8(chosen, t), ALU.add).then_inc(s_before, 1)

            def unit_a(u):
                peeled = isinstance(u, int)
                routes = not peeled or 1 <= u <= UA
                if not peeled or u >= 1:
                    low_gT(u - 1, 0)
                if not peeled or u >= 2:
                    y = shared_y(u - 2, u - 2)
                    if not routes:
                        y.then_inc(s_y, 1)
                if routes:
                    if peeled and u == 1:
                        dve.wait_ge(s_up[1], 1)
                        dve.tensor_copy(logit[:, :], bank[7][:, D:D + E]).then_inc(s_y, 1)
                    else:
                        dve.wait_ge(s_m8, u - 1)
                        at_least(dve, s_i8, u - 1)
                        dve.tensor_copy(logit[:, :], bank[7][:, D:D + E]).then_inc(s_y, 1)
                    dve.wait_ge(s_y, u)
                    if not peeled or u >= 2:
                        dve.wait_ge(s_i2f, u - 1)
                product(u, 0)
                if routes:
                    dve.max(m8[:, :], logit[:, :]).then_inc(s_m8, 1)
                if not peeled or u >= 1:
                    if routes:
                        dve.wait_ge(s_m8, u)
                    low_gT(u - 1, 1)
                if routes:
                    dve.max_index(i8[:, :], m8[:, :], logit[:, :]).then_inc(s_i8, 1)
                low_xT(u + 1)
                if routes:
                    at_least(dve, s_oh, 2 * (u - 1))
                    own_wait(dve, s_i8, u)
                    dve.tensor_copy(i2f[:, :], i8[:, 0:2])
                    dve.tensor_copy(tile8(m8_all, u - 1), m8[:, :]).then_inc(s_i2f, 1)
                product(u, 1)
                if routes:
                    dve.wait_ge(s_i2f, u)
                    dve.tensor_scalar(tile8(oh1, u - 1), iota8, i2f[:, 0:1], None, ALU.is_equal).then_inc(s_oh, 1)
                    dve.tensor_scalar(tile8(oh2, u - 1), iota8, i2f[:, 1:2], None, ALU.is_equal).then_inc(s_oh, 1)
                    count(u - 1)

            def unit_b(u):
                low_gT(u - 1, 0)
                shared_y(u - 2, u - 2 - UA).then_inc(s_y, 1)
                product(u, 0)
                low_gT(u - 1, 1)
                low_xT(u + 1)
                product(u, 1)

            def unit_c(u, last=False):
                low_gT(u - 1, 0)
                routed_y(u - 2)
                product(u, 0)
                low_gT(u - 1, 1)
                if not last:
                    low_xT(u + 1)
                product(u, 1)

            chain = [0]

            def step(ins):
                chain[0] += 1
                ins.then_inc(s_r, 1)
                dve.wait_ge(s_r, chain[0])

            def by_tile(buf):
                return buf[:, :].rearrange("p (t e) -> p t e", e=E)

            def over_tiles(buf, n=TILES, parts=P):
                return buf.unsqueeze(1).to_broadcast([parts, n, E])

            def route_1():
                dve.wait_ge(s_rank, 1)
                dve.tensor_copy(pos_e[:, :], bank[6][:, 0:TILES * E])
                dve.tensor_scalar(n_i[:, :], bank[6][:, TILES * E:(TILES + 1) * E], float(P - 1), None,
                                  ALU.add).then_inc(s_rank_read, 1)
                dve.wait_ge(s_rank_read, 1)
                step(dve.tensor_scalar(n_t[:, :], n_i[:, :], 7, None, ALU.arith_shift_right))
                step(dve.tensor_copy(tiles_f[:, :], n_t[:, :]))
                step(dve.tensor_tensor_scan(end_f[:, :], ones8[:, :], tiles_f[:, :], 0.0, ALU.mult, ALU.add))
                step(dve.tensor_tensor(start_f[:, :], end_f[:, :], tiles_f[:, :], ALU.subtract))

            def route_2():
                dve.wait_ge(s_exp, 1)
                step(dve.scalar_tensor_tensor(out=by_tile(pos_e), in0=over_tiles(start_f[:, :]), scalar=float(P),
                                              in1=by_tile(pos_e), op0=ALU.mult, op1=ALU.add))
                for oh, pos_f, pos in ((oh1, pos1f, pos1), (oh2, pos2f, pos2)):
                    step(dve.tensor_tensor(tmp1[:, :], oh[:, :], pos_e[:, :], ALU.mult))
                    step(dve.tensor_reduce(pos_f[:, :], by_tile(tmp1), AX_X, ALU.add))
                    dve.tensor_copy(pos[:, :], pos_f[:, :]).then_inc(s_pos, 1)
                step(dve.memset(ones_s[:, :], 1.0))

            def route_0():
                dve.wait_ge(s_before, UA + 1)
                dve.tensor_tensor(by_tile(tmp1), by_tile(m8_all),
                                  m8_all[:, 0::E].unsqueeze(2).to_broadcast([P, TILES, E]), ALU.subtract).then_inc(s_dlog, 1)

            def route_3():
                step(dve.tensor_reduce(esum[:, :], by_tile(tmp2), AX_X, ALU.add))
                step(dve.reciprocal(esum[:, :], esum[:, :]))
                step(dve.tensor_tensor(w2[:, :], esum[:, :], tmp2[:, 1::E], ALU.mult))
                dve.tensor_tensor(xn2_all[:, W_COL::ROW], esum[:, :], tmp2[:, 0::E], ALU.mult).then_inc(s_w1, 1)

            def route_4():
                iota_s = consts[0:1, IOTA_S:IOTA_S + SLOTS].unsqueeze(2).to_broadcast([1, SLOTS, E])
                ends = over_tiles(end_f[0:1, :], SLOTS, 1)
                a8 = slot8a[:, :].rearrange("p (s e) -> p s e", e=E)
                b8 = slot8b[:, :].rearrange("p (s e) -> p s e", e=E)
                step(dve.tensor_tensor(a8, ends, iota_s, ALU.is_le))
                step(dve.tensor_reduce(e_of[:, 1:], a8, AX_X, ALU.add))
                step(dve.tensor_scalar(e_of[:, 1:], e_of[:, 1:], float(E - 1), None, ALU.min))
                step(dve.scalar_tensor_tensor(out=b8, in0=a8, scalar=1024.0, in1=ends, op0=ALU.mult, op1=ALU.add))
                step(dve.tensor_reduce(end_of[:, :], b8, AX_X, ALU.min))

            def route_5():
                ends = over_tiles(end_f[0:1, :], SLOTS, 1)
                a8 = slot8a[:, :].rearrange("p (s e) -> p s e", e=E)
                step(dve.tensor_tensor(a8, ends, end_of[:, :].unsqueeze(2).to_broadcast([1, SLOTS, E]), ALU.is_le))
                step(dve.tensor_reduce(next_of[:, :], a8, AX_X, ALU.add))
                step(dve.tensor_scalar(next_i[:, :], next_of[:, :], float(E - 1), None, ALU.min))
                step(dve.tensor_copy(e0_i[:, :], e_of[:, 1:2]))
                step(dve.tensor_tensor(first_of[:, :], e_of[:, 1:], e_of[:, 0:SLOTS], ALU.not_equal))
                step(dve.tensor_tensor_scan(run_of[:, 1:], ones_s[:, :], first_of[:, :], 0.0, ALU.mult, ALU.add))

            def route_6():
                step(dve.tensor_copy(run_i[:, :], run_of[:, :]))
                step(dve.tensor_scalar(par_i[:, :], run_i[:, :], 1, None, ALU.bitwise_and))
                step(dve.tensor_scalar(par_i[:, :], par_i[:, :], -1.0, 1.0, ALU.mult, ALU.add))
                step(dve.scalar_tensor_tensor(out=flag_of[:, :], in0=e_of[:, 1:], scalar=float(E - 1), in1=first_of[:, :],
                                              op0=ALU.is_lt, op1=ALU.mult))
                step(dve.tensor_copy(flag_i[:, :], flag_of[:, :]))
                step(dve.tensor_tensor(fetch_i[0][:, :], flag_i[:, :], par_i[:, 1:], ALU.mult))
                dve.tensor_tensor(fetch_i[1][:, :], flag_i[:, :], fetch_i[0][:, :], ALU.subtract).then_inc(s_tables, 1)

            def route_7():
                dve.wait_ge(s_sort1, 16 * TILES)
                dve.tensor_copy(xn2_all[:, W_COL::ROW], w2[:, :]).then_inc(s_w2, 1)

            dve.wait_ge(s_acc, TILES)
            dve.memset(tile8(before, 0), 0.0).then_inc(s_before, 1)
            dve.memset(ones8[:, :], 1.0)
            dve.memset(e_of[:, 0:1], -1.0)
            dve.memset(run_of[:, 0:1], 0.0)
            low_xT(0)
            for u in range(3):
                unit_a(u)
            with dve.Fori(3, UA) as u:
                unit_a(u)
            unit_a(UA)
            route_0()
            unit_a(UA + 1)
            routing = [route_1, route_2, route_3, route_4, route_5, route_6]
            for k, stage in enumerate(routing):
                stage()
                unit_b(UA + 2 + k)
            with dve.Fori(UA + 2 + len(routing), UB - 15) as u:
                unit_b(u)
            route_7()
            with dve.Fori(UB - 15, UB) as u:
                unit_b(u)
            unit_b(UB)
            unit_b(UB + 1)
            for u in range(UB + 2, UB + 2 + RING):
                unit_c(u)
            with dve.Fori(UB + 2 + RING, UNITS - 1) as u:
                unit_c(u)
            unit_c(UNITS - 1, last=True)
            low_gT(UNITS - 1, 0)
            routed_y(UNITS - 2)
            low_gT(UNITS - 1, 1)
            routed_y(UNITS - 1)

        @block.tensor
        def _(pe):
            def transposes(dst, src, n):
                for c in range(n):
                    mm = pe.transpose(dst[:, c * P:(c + 1) * P], src[:, c * P:(c + 1) * P], ident)
                return mm

            def support(t):
                if not isinstance(t, int) or t >= 1:
                    pe.wait_ge(s_xnl, t)
                    if isinstance(t, int) and t == 1:
                        pe.wait_ge(s_wg, 2)
                    at_least(pe, s_sl, t - 1)
                    k = 0
                    for c in range(DC):
                        high, low = xnT_h[:, c * P:(c + 1) * P], xnT_l[:, c * P:(c + 1) * P]
                        wh, wl = w_gnn_h[:, c * D:(c + 1) * D], w_gnn_l[:, c * D:(c + 1) * D]
                        for a, b in ((high, wh), (high, wl), (low, wh)):
                            mm = pe.matmul(bank[2][:, 0:D], a, b, start=(k == 0), stop=(k == 3 * DC - 1))
                            k += 1
                    mm.then_inc(s_smm, 1)
                if not isinstance(t, int) or t < TILES:
                    pe.wait_ge(s_xn, t + 1)
                    at_least(pe, s_xnl, t)
                    transposes(bank[0], xn, DC).then_inc(s_xnT, 1)

            pe.wait_ge(s_cst, 16)
            for t in range(2):
                support(t)
            with pe.Fori(2, TILES) as t:
                support(t)
            support(TILES)

            def row_block(t, acc):
                at_least(pe, s_x1, t - 1)
                for h in range(2):
                    pe.wait_ge(s_al, 2 * t + h + 1)
                    for k in range(HALF_J):
                        j = h * HALF_J + k
                        high, low = adj_h[h][:, k * P:(k + 1) * P], adj_l[h][:, k * P:(k + 1) * P]
                        pe.matmul(acc[:, 0:2 * D], high, s_hl[:, j * 2 * D:(j + 1) * 2 * D], start=(j == 0), stop=False)
                        mm = pe.matmul(acc[:, D:2 * D], low, s_hl[:, j * 2 * D:j * 2 * D + D], start=False,
                                       stop=(j == TILES - 1))
                    mm.then_inc(s_half[h], 1)

            pe.wait_ge(s_sl, TILES)
            row_block(0, bank[4])
            row_block(1, bank[5])
            with pe.Fori(1, TILES // 2) as pair:
                row_block(2 * pair, bank[4])
                row_block(2 * pair + 1, bank[5])

            def w_part(buffer, low, part):
                def at(col, n):
                    return W[:, bass.ds(buffer * (2 * WCOLS) + (low * WCOLS + part * PART + col), n)]
                return at

            def xT_of(u):
                pe.wait_ge(s_xt, 16 * u + 16)
                at_least(pe, s_xTl, u)
                transposes(bank[6], xt, DC).then_inc(s_xT, 1)

            def up(u, h, buffer):
                pe.wait_ge(s_xTl, u + 1)
                at_least(pe, s_g[h], u)
                for part, dst in ((0, bank[2 * h]), (1, bank[2 * h + 1])):
                    k = 0
                    for c in range(DC):
                        high, low = xT_h[:, c * P:(c + 1) * P], xT_l[:, c * P:(c + 1) * P]
                        col = c * HID + h * HALF
                        for a, b in ((high, 0), (high, 1), (low, 0)):
                            mm = pe.matmul(dst[:, 0:HALF], a, w_part(buffer, b, part)(col, HALF), start=(k == 0),
                                           stop=(k == 3 * DC - 1))
                            k += 1
                mm.then_inc(s_up[h], 1)

            def turn(u, h):
                pe.wait_ge(s_g[h], u + 1)
                at_least(pe, s_gTl[h], u)
                transposes(bank[4 + h], g[h], HC // 2).then_inc(s_gT[h], 1)

            def down(u, h, buffer):
                pe.wait_ge(s_gTl[h], u + 1)
                if h == 0:
                    at_least(pe, s_y, u + 1)
                for k in range(HC // 2):
                    high, low = gT_h[h][:, k * P:(k + 1) * P], gT_l[h][:, k * P:(k + 1) * P]
                    col = (h * (HC // 2) + k) * D
                    for n, (a, b) in enumerate(((high, 0), (high, 1), (low, 0))):
                        mm = pe.matmul(bank[7][:, 0:D], a, w_part(buffer, b, 2)(col, D), start=(h == 0 and k == 0 and n == 0),
                                       stop=(h == 1 and k == HC // 2 - 1 and n == 2))
                if h == 1:
                    mm.then_inc(s_down, 1)

            def logits(u):
                at_least(pe, s_y, u)
                k = 0
                for c in range(DC):
                    high, low = xT_h[:, c * P:(c + 1) * P], xT_l[:, c * P:(c + 1) * P]
                    gh, gl = gate_h[:, c * E:(c + 1) * E], gate_l[:, c * E:(c + 1) * E]
                    for a, b in ((high, gh), (high, gl), (low, gh)):
                        pe.matmul(bank[7][:, D:D + E], a, b, start=(k == 0), stop=(k == 3 * DC - 1))
                        k += 1

            def ranks():
                pe.wait_ge(s_before, UA + 1)
                pe.matmul(bank[6][:, 0:TILES * E], tri, chosen[:, :], start=True, stop=False, skip_group_check=True)
                pe.matmul(bank[6][:, 0:TILES * E], ones_pp, before[:, 0:TILES * E], start=False, stop=True, skip_group_check=True)
                pe.matmul(bank[6][:, TILES * E:(TILES + 1) * E], ones_pp, before[:, TILES * E:(TILES + 1) * E], start=False,
                          stop=True, skip_group_check=True).then_inc(s_rank, 1)

            def unit(u, buffer, buffer_before, gate_too=False, last=False, rank=False, whole=None, whole_before=None):
                first = isinstance(u, int) and u == 0
                if whole is not None:
                    pe.wait_ge(s_wl, whole - 1)
                up(u, 0, buffer)
                if not first:
                    turn(u - 1, 1)
                if rank:
                    ranks()
                    pe.wait_ge(s_rank_read, 1)
                if not last:
                    xT_of(u + 1)
                if gate_too:
                    logits(u)
                up(u, 1, buffer)
                if not first:
                    if whole_before is not None:
                        pe.wait_ge(s_wl, whole_before)
                    down(u - 1, 0, buffer_before)
                turn(u, 0)
                if not first:
                    down(u - 1, 1, buffer_before)

            pe.wait_ge(s_gate, 2)
            xT_of(0)
            unit(0, 0, 0, gate_too=True, whole=3)
            unit(1, 0, 0, gate_too=True, whole_before=3)
            with pe.Fori(2, UA) as u:
                unit(u, 0, 0, gate_too=True)
            unit(UA, 1, 0, whole=6)
            unit(UA + 1, 1, 1, whole_before=6)
            unit(UA + 2, 1, 1, rank=True)
            with pe.Fori(UA + 3, UB) as u:
                unit(u, 1, 1)
            pe.wait_ge(s_tables, 1)

            def routed(s, last=False):
                run = pe.value_load(run_i[0:1, bass.ds(s + 1, 1)], min_val=1, max_val=E)
                run_before = pe.value_load(run_i[0:1, bass.ds(s, 1)], min_val=0, max_val=E)
                par = pe.value_load(par_i[0:1, bass.ds(s + 1, 1)], min_val=0, max_val=1)
                par_before = pe.value_load(par_i[0:1, bass.ds(s, 1)], min_val=0, max_val=1)
                unit(s + UB, par, par_before, whole=run * 3 + 6, whole_before=run_before * 3 + 6, last=last)

            with pe.Fori(0, SLOTS - 1) as s:
                routed(s)
            routed(SLOTS - 1, last=True)
            par = pe.value_load(par_i[0:1, SLOTS:SLOTS + 1], min_val=0, max_val=1)
            turn(UNITS - 1, 1)
            down(UNITS - 1, 0, par)
            down(UNITS - 1, 1, par)


def kernel(x, adj, L0_gnn_weight, L0_gnn_bias, L0_ffn_gate_w, L0_ffn_w1, L0_ffn_w3, L0_ffn_w2,
           L0_ffn_sw1, L0_ffn_sw3, L0_ffn_sw2):
    import concourse.bacc as bacc
    from concourse.bass_utils import run_bass_kernel_spmd

    def np32(a):
        return np.asarray(a, dtype=np.float32)

    def features_on_partitions(w):
        return np.ascontiguousarray(w.T.reshape(DC, P, -1).transpose(1, 0, 2)).reshape(P, -1)

    x, adj = np32(x), np32(adj)
    pad = NP - N
    x_in = np.pad(x, ((0, pad), (0, 0))).reshape(TILES, P, D).transpose(1, 0, 2).reshape(P, TILES * D)
    adj_p = np.pad(adj, ((0, pad), (0, pad))).reshape(TILES, P, TILES, P)
    adj_in = np.ascontiguousarray(adj_p.transpose(0, 3, 2, 1)).reshape(TILES * P, TILES * P)
    w_in = np32(L0_gnn_weight).reshape(DC, P, D).transpose(1, 0, 2).reshape(P, DC * D)
    bias_in = np.tile(np32(L0_gnn_bias)[None, :], (P, 1))
    gate_in = features_on_partitions(np32(L0_ffn_gate_w))
    sw1, sw3, sw2 = np32(L0_ffn_sw1), np32(L0_ffn_sw3), np32(L0_ffn_sw2)
    w1 = list(sw1.reshape(2, HID, D)) + list(np32(L0_ffn_w1))
    w3 = list(sw3.reshape(2, HID, D)) + list(np32(L0_ffn_w3))
    w2 = [sw2[:, :HID], sw2[:, HID:]] + list(np32(L0_ffn_w2))
    down = [np.ascontiguousarray(w.T.reshape(HC, P, D).transpose(1, 0, 2)).reshape(P, -1) for w in w2]
    experts_in = np.stack([m for a, b, c in zip(w1, w3, down)
                           for m in (features_on_partitions(a), features_on_partitions(b), c)]).reshape(-1, PART)
    cst = np.zeros((P, CST), np.float32)
    cst[:, IDENT:IDENT + P] = np.eye(P)
    cst[:, TRI:TRI + P] = np.triu(np.ones((P, P)), 1)
    cst[:, IOTA8:IOTA8 + E] = np.arange(E)
    cst[:, ONES:ONES + P] = 1
    cst[:, IOTA_S:IOTA_S + SLOTS] = np.arange(SLOTS)

    nc = bacc.Bacc("TRN2", target_bir_lowering=False, num_devices=1)
    arrays = {"x_in": x_in, "adj_in": adj_in, "w_in": w_in, "bias_in": bias_in, "gate_in": gate_in,
              "experts_in": experts_in, "cst_in": cst}
    arrays = {k: np.ascontiguousarray(v) for k, v in arrays.items()}
    args = [nc.dram_tensor(k, list(v.shape), F32, kind="ExternalInput").ap() for k, v in arrays.items()]
    out = nc.dram_tensor("out", [NP + P, D], F32, kind="ExternalOutput").ap()
    build(nc, *args, out)
    r = run_bass_kernel_spmd(nc, [arrays], core_ids=[0])
    return r.results[0]["out"][:N]
```

```python
from contextlib import ExitStack

import numpy as np

import concourse.bass as bass
from concourse import mybir

F32 = mybir.dt.float32
F32R = mybir.dt.float32r
I32 = mybir.dt.int32
U32 = mybir.dt.uint32
ALU = mybir.AluOpType
ACT = mybir.ActivationFunctionType
AX_X = mybir.AxisListType.X

P = 128
N = 3327
D = 256
DC = D // P
E = 8
HID = 768
HC = HID // P
HALF = HID // 2
TILES = -(-N // P)
NP = TILES * P
HALF_J = TILES // 2
UA = TILES
UB = 2 * TILES
SLOTS = (2 * NP) // P + E - 1
UNITS = UB + SLOTS
ROW = D + 4
ID_COL, W_COL = D, D + 1
W1_COLS = HID + E
PARTS = (DC * W1_COLS, DC * HID, HC * D)
PART_AT = (0, PARTS[0], PARTS[0] + PARTS[1])
WCOLS = sum(PARTS)
RUN0_LEAD = 14
RING = 4
EPS = 1e-5
IDENT, TRI, ONES, IOTA8, IOTA_S = 0, P, 2 * P, 3 * P, 3 * P + E
CST = IOTA_S + SLOTS


def at_least(eng, sem, value):
    if isinstance(value, int) and value <= 0:
        return
    eng.wait_ge(sem, value)


def build(nc, x, adj, w_gnn, bias, weights, cst, out):
    xn_dram = nc.dram_tensor("xn_dram", [NP, ROW], F32, kind="Internal").ap()
    sorted_dram = nc.dram_tensor("sorted_dram", [SLOTS * P, ROW], F32, kind="Internal").ap()

    place = [-(-nc.sbuf_base // 32) * 32]

    def sb(name, cols, dt=F32, parts=P):
        t = nc.alloc_sbuf_tensor_at(name, [parts, cols], dt, offset=place[0])
        place[0] += -(-cols * 4 // 32) * 32
        return t

    ctx = ExitStack()
    with ctx:
        x_all = sb("x_all", TILES * D)
        xn2_all = sb("xn2_all", TILES * ROW)
        raw_w = sb("raw_w", WCOLS)
        consts = sb("consts", CST)
        small = sb("small", 32)
        sd_all = sb("sd_all", TILES)
        rs_all = sb("rs_all", TILES)
        zrow = sb("zrow", ROW)
        meta_id = sb("meta_id", RING, I32)
        meta_w = sb("meta_w", RING)
        xt = sb("xt", ROW)
        xT_h = sb("xT_h", D, F32R)
        xT_l = sb("xT_l", D, F32R)
        w_start = place[0]
        W = nc.alloc_sbuf_tensor_at("W", [P, 2 * 2 * WCOLS], F32R, offset=w_start)
        first_layer = w_start + 2 * WCOLS * 4
        place[0] = first_layer
        s_hl = sb("s_hl", TILES * 2 * D, F32R)
        adj_raw = [sb(f"adj_raw{h}", HALF_J * P) for h in range(2)]
        adj_h, adj_l = [], []
        for h in range(2):
            support_only = place[0]
            adj_h.append(sb(f"adj_h{h}", HALF_J * P, F32R))
            adj_l.append(sb(f"adj_l{h}", HALF_J * P, F32R))
        bias_sb = sb("bias_sb", D)
        assert place[0] <= nc.sbuf_usable_end, (place[0], nc.sbuf_usable_end)
        place[0] = support_only
        w_gnn_raw = sb("w_gnn_raw", DC * D)
        w_gnn_h = sb("w_gnn_h", DC * D, F32R)
        w_gnn_l = sb("w_gnn_l", DC * D, F32R)
        xc = [sb(f"xc{b}", D) for b in range(2)]
        xcT_h = [sb(f"xcT_h{b}", D, F32R) for b in range(2)]
        xcT_l = [sb(f"xcT_l{b}", D, F32R) for b in range(2)]
        assert place[0] <= support_only + 2 * HALF_J * P * 4
        place[0] = first_layer + 2 * WCOLS * 4
        sil = [sb(f"sil{h}", HALF) for h in range(2)]
        g = [sb(f"g{h}", HALF) for h in range(2)]
        gT_h = [sb(f"gT_h{h}", HALF, F32R) for h in range(2)]
        gT_l = [sb(f"gT_l{h}", HALF, F32R) for h in range(2)]
        y_ring = sb("y_ring", RING * D)
        id_ring = sb("id_ring", RING, I32)
        logit = sb("logit", E)
        m8 = sb("m8", E)
        i8 = sb("i8", E, U32)
        i2f = sb("i2f", 2)
        m8_all = sb("m8_all", TILES * E)
        oh1 = sb("oh1", TILES * E)
        oh2 = sb("oh2", TILES * E)
        chosen = sb("chosen", TILES * E)
        before = sb("before", (TILES + 1) * E)
        pos_e = sb("pos_e", TILES * E)
        tmp1 = sb("tmp1", TILES * E)
        tmp2 = sb("tmp2", TILES * E)
        esum = sb("esum", TILES)
        w2 = sb("w2", TILES)
        pos1f = sb("pos1f", TILES)
        pos2f = sb("pos2f", TILES)
        pos1 = sb("pos1", TILES, I32)
        pos2 = sb("pos2", TILES, I32)
        n_i = sb("n_i", E, I32)
        n_t = sb("n_t", E, I32)
        tiles_f = sb("tiles_f", E)
        ones8 = sb("ones8", E)
        end_f = sb("end_f", E)
        start_f = sb("start_f", E)
        slot8a = sb("slot8a", SLOTS * E, parts=1)
        slot8b = sb("slot8b", SLOTS * E, parts=1)
        e_of = sb("e_of", SLOTS + 1, parts=1)
        end_of = sb("end_of", SLOTS, parts=1)
        next_of = sb("next_of", SLOTS, parts=1)
        first_of = sb("first_of", SLOTS, parts=1)
        ones_s = sb("ones_s", SLOTS, parts=1)
        run_of = sb("run_of", SLOTS + 1, parts=1)
        flag_of = sb("flag_of", SLOTS, parts=1)
        run_i = sb("run_i", SLOTS + 1, I32, parts=1)
        par_i = sb("par_i", SLOTS + 1, I32, parts=1)
        runs_i = sb("runs_i", SLOTS, I32, parts=1)
        flag_i = sb("flag_i", SLOTS, I32, parts=1)
        fetch_i = [sb(f"fetch_i{b}", SLOTS, I32, parts=1) for b in range(2)]
        next_i = sb("next_i", SLOTS, I32, parts=1)
        e0_i = sb("e0_i", 1, I32, parts=1)
        assert place[0] <= nc.sbuf_usable_end
        bank = [ctx.enter_context(nc.psum_tensor(f"bank{b}", [P, 512], F32)) for b in range(8)]

        st, mv = [small[:, 0:6], small[:, 26:32]], [small[:, 6:8], small[:, 8:10]]
        eps = small[:, 10:11]
        st2, mv2, sd2, rs2 = small[:, 16:22], small[:, 22:24], small[:, 24:25], small[:, 25:26]
        ident = consts[:, IDENT:IDENT + P]
        tri = consts[:, TRI:TRI + P]
        ones_pp = consts[:, ONES:ONES + P]
        iota8 = consts[:, IOTA8:IOTA8 + E]

        def sem(name):
            return ctx.enter_context(nc.semaphore(name))

        s_x = [sem("s_x_in0"), sem("s_x_in1")]; s_small_in = sem("s_small_in"); s_cst = sem("s_cst"); s_bias = sem("s_bias");
        s_adj = [sem("s_adj0"), sem("s_adj1")]
        s_raw_w = [sem(f"s_raw_w{i}") for i in range(3)]
        s_prefill = sem("s_prefill"); s_trash = sem("s_trash"); s_xn_out = sem("s_xn_out"); s_xt = sem("s_xt")
        s_sort1 = sem("s_sort1"); s_sort2 = sem("s_sort2"); s_out = sem("s_out"); s_add = sem("s_add")
        s_passed = sem("s_passed"); s_eps = sem("s_eps"); s_zero = sem("s_zero"); s_zid = sem("s_zid"); s_wg = sem("s_wg"); s_ids = sem("s_ids"); s_init = sem("s_init")
        s_bn = sem("s_bn"); s_mv = sem("s_mv"); s_sd = sem("s_sd"); s_rs = sem("s_rs"); s_xc = sem("s_xc")
        s_xT1 = sem("s_xT1"); s_xch = sem("s_xch"); s_xcl = sem("s_xcl"); s_smm = sem("s_smm"); s_sh = sem("s_sh"); s_sl = sem("s_sl")
        s_biased = sem("s_biased")
        s_ah = sem("s_ah"); s_al = sem("s_al"); s_half = [sem("s_half0"), sem("s_half1")]; s_acc = s_half[1]
        s_t1 = sem("s_t1"); s_x1 = sem("s_x1"); s_bn2 = sem("s_bn2"); s_mv2 = sem("s_mv2"); s_sd2 = sem("s_sd2"); s_rs2 = sem("s_rs2"); s_xn2 = sem("s_xn2")
        s_wh = sem("s_wh"); s_wl = sem("s_wl")
        s_xT = sem("s_xT"); s_xTh = sem("s_xTh"); s_xTl = sem("s_xTl"); s_meta = sem("s_meta")
        s_up = [sem("s_up0"), sem("s_up1")]; s_sil = [sem("s_sil0"), sem("s_sil1")]; s_g = [sem("s_g0"), sem("s_g1")]
        s_gT = [sem("s_gT0"), sem("s_gT1")]; s_gTh = [sem("s_gTh0"), sem("s_gTh1")]; s_gTl = [sem("s_gTl0"), sem("s_gTl1")]
        s_down = sem("s_down"); s_y = sem("s_y")
        s_logit = sem("s_logit"); s_m8 = sem("s_m8"); s_i8 = sem("s_i8"); s_i2f = sem("s_i2f"); s_oh = sem("s_oh"); s_chosen = sem("s_chosen"); s_before = sem("s_before")
        s_rank = sem("s_rank"); s_rank_read = sem("s_rank_read"); s_dlog = sem("s_dlog"); s_exp = sem("s_exp")
        s_r = sem("s_r"); s_pos = sem("s_pos"); s_w1 = sem("s_w1"); s_w2 = sem("s_w2"); s_tables = sem("s_tables")

        block = ctx.enter_context(nc.Block())

        def own_wait(eng, sem, value):
            at_least(eng, sem, value)
            if not isinstance(value, int):
                eng.sem_inc(s_passed, 1)

        def rows(t):
            return bass.ds(t * P, P)

        def xtile(t):
            return x_all[:, bass.ds(t * D, D)]

        def load_expert(eng, e, n):
            for part in range(3):
                at_least(eng, s_wl, 3 * (n - 1) + part + 1)
                at, cols = PART_AT[part], PARTS[part]
                eng.dma_start(raw_w[:, at:at + cols], weights[rows(e), at:at + cols]).then_inc(s_raw_w[part], 16)

        @block.sync
        def _(sp):
            sp.dma_start(x_all[:, 0:2 * D], x[:, 0:2 * D]).then_inc(s_x[0], 16)
            sp.dma_start(w_gnn_raw[:, :], w_gnn).then_inc(s_small_in, 16)
            sp.dma_start(consts[:, :], cst).then_inc(s_cst, 16)
            sp.dma_start(x_all[:, 2 * D:], x[:, 2 * D:]).then_inc(s_x[1], 16)
            sp.dma_start(bias_sb[:, :], bias).then_inc(s_bias, 16)

            def adj_load(t, h):
                at_least(sp, s_al, 2 * t - 1 + h)
                sp.dma_start(adj_raw[h][:, :], adj[rows(t), h * HALF_J * P:(h + 1) * HALF_J * P]).then_inc(s_adj[h], 16)

            def xn_store(t):
                sp.wait_ge(s_xn2, t + 1)
                at_least(sp, s_xn_out, 16 * t)
                sp.dma_start(xn_dram[rows(t), :], xn2_all[:, bass.ds(t * ROW, ROW)]).then_inc(s_xn_out, 16)

            def unit_load(u, source, tile):
                at_least(sp, s_xT, u)
                at_least(sp, s_meta, u)
                sp.dma_start(xt[:, :], source[rows(tile), :]).then_inc(s_xt, 16)

            def out_store(u):
                sp.wait_ge(s_y, u + 1)
                sp.dma_start(out[rows(u - UA), :], xtile(u - UA)).then_inc(s_out, 16)

            for t in range(2):
                for h in range(2):
                    adj_load(t, h)
                if t == 0:
                    load_expert(sp, 0, 0)
            sp.wait_ge(s_ids, TILES)
            sp.wait_ge(s_init, 1)
            with sp.Fori(2, 3) as t:
                adj_load(t, 0)
                adj_load(t, 1)
            xn_store(0)
            with sp.Fori(3, TILES) as t:
                adj_load(t, 0)
                adj_load(t, 1)
                xn_store(t - 2)
            unit_load(0, xn_dram, 0)
            xn_store(TILES - 2)
            xn_store(TILES - 1)
            sp.wait_ge(s_xn_out, 16 * TILES)
            unit_load(1, xn_dram, 1)
            load_expert(sp, 1, 1)
            with sp.Fori(2, UA) as u:
                unit_load(u, xn_dram, u)
            for u in range(UA, UA + 4):
                unit_load(u, xn_dram, u - UA)
            with sp.Fori(UA + 4, UB - RUN0_LEAD) as u:
                unit_load(u, xn_dram, u - UA)
                out_store(u - 4)
            sp.wait_ge(s_tables, 1)
            load_expert(sp, sp.value_load(e0_i[0:1, 0:1], min_val=0, max_val=E - 1) + 2, 2)
            with sp.Fori(UB - RUN0_LEAD, UB) as u:
                unit_load(u, xn_dram, u - UA)
                out_store(u - 4)
            sp.wait_ge(s_sort1, 16 * TILES)
            sp.wait_ge(s_sort2, 16 * TILES)

            def fetch(s):
                flag = sp.value_load(flag_i[0:1, bass.ds(s, 1)], min_val=0, max_val=1)
                with sp.If(flag > 0):
                    e = sp.value_load(next_i[0:1, bass.ds(s, 1)], min_val=0, max_val=E - 1)
                    run1 = sp.value_load(run_i[0:1, bass.ds(s + 1, 1)], min_val=1, max_val=E)
                    load_expert(sp, e + 2, run1 + 2)

            for s in range(4):
                unit_load(UB + s, sorted_dram, s)
                out_store(UB - 4 + s)
                if s >= 2:
                    fetch(s - 2)
            with sp.Fori(4, SLOTS) as s:
                unit_load(UB + s, sorted_dram, s)
                fetch(s - 2)
            for s in range(SLOTS - 2, SLOTS):
                fetch(s)

        @block.gpsimd
        def _(pool):
            pool.memset(zrow[:, :], 0.0).then_inc(s_zero, 1)
            pool.memset(xn2_all[:, :], 0.0).then_inc(s_init, 1)
            pool.wait_ge(s_zero, 1)
            pool.iota(zrow[:, ID_COL:ID_COL + 1].bitcast(I32), [[0, 1]], base=NP, channel_multiplier=1).then_inc(s_zid, 1)
            pool.wait_ge(s_zid, 1)
            pool.wait_ge(s_init, 1)
            for t in range(TILES):
                pool.iota(xn2_all[:, t * ROW + ID_COL:t * ROW + ID_COL + 1].bitcast(I32), [[0, 1]], base=t * P,
                          channel_multiplier=1).then_inc(s_ids, 1)
            def centre(t, b):
                at_least(pool, s_xT1, t - 1)
                own_wait(pool, s_mv, t + 1)
                pool.tensor_tensor(xc[b][:, :], xtile(t), mv[b][:, 0:1].to_broadcast([P, D]), ALU.subtract).then_inc(s_xc, 1)
                if isinstance(t, int) and t == 0:
                    pool.wait_ge(s_bias, 16)
                own_wait(pool, s_xc, t + 1)
                pool.tensor_tensor(xtile(t), xtile(t), bias_sb[:, :], ALU.add).then_inc(s_biased, 1)

            centre(0, 0)
            centre(1, 1)
            with pool.Fori(1, TILES // 2) as pair:
                centre(2 * pair, 0)
                centre(2 * pair + 1, 1)
            pool.dma_start(out[rows(TILES), :], zrow[:, 0:D]).then_inc(s_trash, 16)
            with pool.Fori(0, SLOTS) as s:
                pool.dma_start(sorted_dram[rows(s), :], zrow[:, :]).then_inc(s_prefill, 16)

            def split_expert(n, buffer):
                for part in range(3):
                    at, cols = PART_AT[part], PARTS[part]
                    high = W[:, buffer * 2 * WCOLS + at:buffer * 2 * WCOLS + at + cols]
                    low = W[:, (buffer * 2 + 1) * WCOLS + at:(buffer * 2 + 1) * WCOLS + at + cols]
                    raw = raw_w[:, at:at + cols]
                    own_wait(pool, s_raw_w[part], 16 * (n + 1))
                    pool.tensor_scalar(high, raw, 1.0, 1.0, ALU.mult, ALU.mult).then_inc(s_wh, 1)
                    pool.wait_ge(s_wh, 3 * n + part + 1)
                    pool.tensor_tensor(low, raw, high.bitcast(F32), ALU.subtract).then_inc(s_wl, 1)

            split_expert(0, 0)
            pool.wait_ge(s_acc, TILES)
            split_expert(1, 1)
            pool.wait_ge(s_prefill, 16 * SLOTS)
            for which, (pos, ready, done) in enumerate(((pos1, s_w1, s_sort1), (pos2, s_w2, s_sort2))):
                pool.wait_ge(s_pos, 2)
                pool.wait_ge(ready, 1)
                for t in range(TILES):
                    pool.indirect_dma_start(sorted_dram[:, :], bass.IndirectOffsetOnAxis(ap=pos[:, t:t + 1], axis=0),
                                            xn2_all[:, t * ROW:(t + 1) * ROW], None).then_inc(done, 16)
            pool.wait_ge(s_down, UA)
            split_expert(2, 0)
            pool.wait_ge(s_out, 16 * TILES)
            pool.wait_ge(s_trash, 16)

            def routed_unit(s, slot):
                for buffer in range(2):
                    flag = pool.value_load(fetch_i[buffer][0:1, bass.ds(s, 1)], min_val=0, max_val=1)
                    with pool.If(flag > 0):
                        run1 = pool.value_load(run_i[0:1, bass.ds(s + 1, 1)], min_val=1, max_val=E)
                        own_wait(pool, s_down, s + UB)
                        split_expert(run1 + 2, buffer)
                own_wait(pool, s_y, s + (UB + 1))
                if not isinstance(s, int) or s > 0:
                    own_wait(pool, s_add, s * 16)
                pool.indirect_dma_start(out[:, :], bass.IndirectOffsetOnAxis(ap=id_ring[:, slot:slot + 1], axis=0),
                                        y_ring[:, slot * D:(slot + 1) * D], None, compute_op=ALU.add).then_inc(s_add, 16)

            for s in range(RING):
                routed_unit(s, s)
            with pool.Fori(1, SLOTS // RING) as q:
                for slot in range(RING):
                    routed_unit(q * RING + slot, slot)
            for s in range(SLOTS // RING * RING, SLOTS):
                routed_unit(s, s % RING)
            pool.wait_ge(s_add, 16 * SLOTS)

        @block.scalar
        def _(act):
            def support(t, b):
                peeled = isinstance(t, int)
                if not peeled or 1 <= t <= TILES:
                    act.wait_ge(s_xT1, t)
                    act.activation(xcT_h[1 - b][:, :], bank[1 - b][:, 0:D], ACT.Copy).then_inc(s_xch, 1)
                if not peeled or t >= 2:
                    at_least(act, s_rs, t - 1)
                    own_wait(act, s_smm, t - 1)
                    act.activation(s_hl[:, bass.ds((t - 2) * (2 * D), D)], bank[2 + b][:, 0:D], ACT.Copy,
                                   scale=rs_all[:, bass.ds(t - 2, 1)]).then_inc(s_sh, 1)
                if not peeled or t < TILES:
                    if peeled and t == 0:
                        act.wait_ge(s_eps, 1)
                    own_wait(act, s_mv, t + 1)
                    act.activation(sd_all[:, bass.ds(t, 1)], mv[b][:, 1:2], ACT.Sqrt, bias=eps).then_inc(s_sd, 1)

            support(0, 0)
            support(1, 1)
            with act.Fori(1, TILES // 2) as pair:
                support(2 * pair, 0)
                support(2 * pair + 1, 1)
            support(TILES, 0)
            support(TILES + 1, 1)

            def neighbours(t):
                for h in range(2):
                    act.wait_ge(s_adj[h], 16 * t + 16)
                    at_least(act, s_half[h], t)
                    if isinstance(t, int) and t == 0 and h == 1:
                        act.wait_ge(s_sl, TILES)
                    act.activation(adj_h[h][:, :], adj_raw[h][:, :], ACT.Copy).then_inc(s_ah, 1)
                std(t - 1)

            def std(t):
                if isinstance(t, int) and t < 0:
                    return
                act.wait_ge(s_mv2, t + 1)
                act.activation(sd2, mv2[:, 1:2], ACT.Sqrt, bias=eps).then_inc(s_sd2, 1)

            neighbours(0)
            with act.Fori(1, TILES) as t:
                neighbours(t)
            act.wait_ge(s_xT, 1)
            act.activation(xT_h[:, :], bank[6][:, 0:D], ACT.Copy).then_inc(s_xTh, 1)
            std(TILES - 1)

            def high_gT(u, h):
                act.wait_ge(s_gT[h], u + 1)
                act.activation(gT_h[h][:, :], bank[4 + h][:, 0:HALF], ACT.Copy).then_inc(s_gTh[h], 1)

            def high_xT(u):
                act.wait_ge(s_xT, u + 1)
                at_least(act, s_up[1], u)
                act.activation(xT_h[:, :], bank[6][:, 0:D], ACT.Copy).then_inc(s_xTh, 1)

            def silu(u, h):
                act.wait_ge(s_up[h], u + 1)
                at_least(act, s_g[h], u)
                act.activation(sil[h][:, :], bank[2 * h][:, 0:HALF], ACT.Silu).then_inc(s_sil[h], 1)

            def unit(u, last=False):
                first = isinstance(u, int) and u == 0
                if not first:
                    high_gT(u - 1, 0)
                silu(u, 0)
                if not first:
                    high_gT(u - 1, 1)
                if not last:
                    high_xT(u + 1)
                silu(u, 1)

            unit(0)
            with act.Fori(1, UA + 2) as u:
                unit(u)
            act.wait_ge(s_dlog, 1)
            act.activation(tmp2[:, :], tmp1[:, :], ACT.Exp).then_inc(s_exp, 1)
            act.activation(small[:, 12:13], eps, ACT.Silu)
            with act.Fori(UA + 2, UNITS - 1) as u:
                unit(u)
            unit(UNITS - 1, last=True)
            high_gT(UNITS - 1, 0)
            high_gT(UNITS - 1, 1)

        @block.vector
        def _(dve):
            dve.memset(eps, EPS).then_inc(s_eps, 1)
            dve.wait_ge(s_small_in, 16)
            dve.tensor_copy(w_gnn_h[:, :], w_gnn_raw[:, :]).then_inc(s_wg, 1)
            dve.wait_ge(s_wg, 1)
            dve.tensor_tensor(w_gnn_l[:, :], w_gnn_raw[:, :], w_gnn_h[:, :].bitcast(F32), ALU.subtract).then_inc(s_wg, 1)

            def stats(t, b):
                if isinstance(t, int) and t < 4:
                    dve.wait_ge(s_x[min(t // 2, 1)], 16)
                if not isinstance(t, int) or t >= 2:
                    own_wait(dve, s_mv, t - 1)
                dve.bn_stats(st[b], xtile(t)).then_inc(s_bn, 1)

            def support(t, b):
                peeled = isinstance(t, int)
                if not peeled or t < TILES - 1:
                    stats(t + 1, 1 - b)
                if not peeled or t < TILES:
                    at_least(dve, s_xc, t - 1)
                    at_least(dve, s_sd, t - 1)
                    own_wait(dve, s_bn, t + 1)
                    dve.bn_aggr(mv[b], st[b]).then_inc(s_mv, 1)
                if not peeled or t >= 2:
                    own_wait(dve, s_sh, t - 1)
                    dve.scalar_tensor_tensor(out=s_hl[:, bass.ds((t - 2) * (2 * D) + D, D)], in0=bank[2 + b][:, 0:D],
                                             scalar=rs_all[:, bass.ds(t - 2, 1)],
                                             in1=s_hl[:, bass.ds((t - 2) * (2 * D), D)].bitcast(F32),
                                             op0=ALU.mult, op1=ALU.subtract).then_inc(s_sl, 1)
                if not peeled or 1 <= t <= TILES:
                    own_wait(dve, s_sd, t)
                    dve.reciprocal(rs_all[:, bass.ds(t - 1, 1)], sd_all[:, bass.ds(t - 1, 1)]).then_inc(s_rs, 1)
                    dve.wait_ge(s_xch, t)
                    dve.tensor_tensor(xcT_l[1 - b][:, :], bank[1 - b][:, 0:D], xcT_h[1 - b][:, :].bitcast(F32),
                                      ALU.subtract).then_inc(s_xcl, 1)

            stats(0, 0)
            for t in range(4):
                support(t, t % 2)
            with dve.Fori(2, TILES // 2 - 1) as pair:
                support(2 * pair, 0)
                support(2 * pair + 1, 1)
            for t in range(TILES - 2, TILES + 2):
                support(t, t % 2)

            def low_xT(u):
                own_wait(dve, s_xTh, u + 1)
                dve.tensor_copy(meta_id[:, bass.ds(u % RING, 1)], xt[:, ID_COL:ID_COL + 1].bitcast(I32))
                dve.tensor_copy(meta_w[:, bass.ds(u % RING, 1)], xt[:, W_COL:W_COL + 1]).then_inc(s_meta, 1)
                dve.tensor_tensor(xT_l[:, :], bank[6][:, 0:D], xT_h[:, :].bitcast(F32), ALU.subtract).then_inc(s_xTl, 1)

            def low_adj(t, h):
                dve.wait_ge(s_ah, 2 * t + h + 1)
                dve.tensor_tensor(adj_l[h][:, :], adj_raw[h][:, :], adj_h[h][:, :].bitcast(F32), ALU.subtract).then_inc(s_al, 1)

            def residual(t, acc):
                dve.wait_ge(s_acc, t + 1)
                dve.wait_ge(s_biased, t + 1)
                dve.tensor_tensor(xtile(t), acc[:, 0:D], xtile(t), ALU.add).then_inc(s_t1, 1)
                dve.wait_ge(s_t1, t + 1)
                dve.tensor_tensor(xtile(t), acc[:, D:2 * D], xtile(t), ALU.add).then_inc(s_x1, 1)
                at_least(dve, s_mv2, t)
                own_wait(dve, s_x1, t + 1)
                dve.bn_stats(st2, xtile(t)).then_inc(s_bn2, 1)

            def norm_mean(t):
                at_least(dve, s_xn2, t)
                own_wait(dve, s_bn2, t + 1)
                dve.bn_aggr(mv2, st2).then_inc(s_mv2, 1)

            def norm(t):
                dve.wait_ge(s_sd2, t + 1)
                dve.reciprocal(rs2, sd2).then_inc(s_rs2, 1)
                dve.wait_ge(s_rs2, t + 1)
                if isinstance(t, int) and t == 0:
                    dve.wait_ge(s_init, 1)
                dve.tensor_scalar(xn2_all[:, bass.ds(t * ROW, D)], xtile(t), mv2[:, 0:1], rs2,
                                  ALU.subtract, ALU.mult).then_inc(s_xn2, 1)

            def row_block(t, acc_before):
                low_adj(t, 0)
                low_adj(t, 1)
                if isinstance(t, int) and t == 0:
                    return
                residual(t - 1, acc_before)
                norm_mean(t - 1)
                norm(t - 1)

            row_block(0, None)
            row_block(1, bank[4])
            with dve.Fori(1, TILES // 2) as pair:
                row_block(2 * pair, bank[5])
                row_block(2 * pair + 1, bank[4])
            low_xT(0)
            residual(TILES - 1, bank[5])
            norm_mean(TILES - 1)
            norm(TILES - 1)

            def low_gT(u, h):
                dve.wait_ge(s_gTh[h], u + 1)
                dve.tensor_tensor(gT_l[h][:, :], bank[4 + h][:, 0:HALF], gT_h[h][:, :].bitcast(F32), ALU.subtract).then_inc(s_gTl[h], 1)

            def product(u, h):
                dve.wait_ge(s_sil[h], u + 1)
                at_least(dve, s_gT[h], u)
                dve.tensor_tensor(g[h][:, :], bank[2 * h + 1][:, 0:HALF], sil[h][:, :], ALU.mult).then_inc(s_g[h], 1)

            def shared_y(u, tile):
                dve.wait_ge(s_down, u + 1)
                return dve.tensor_tensor(xtile(tile), bank[7][:, 0:D], xtile(tile), ALU.add)

            def routed_y(u):
                s = u - UB
                r = s % RING
                at_least(dve, s_add, 16 * (s - RING + 1))
                dve.wait_ge(s_meta, u + 1)
                own_wait(dve, s_down, u + 1)
                dve.tensor_copy(id_ring[:, bass.ds(r, 1)], meta_id[:, bass.ds(u % RING, 1)])
                dve.tensor_scalar(y_ring[:, bass.ds(r * D, D)], bank[7][:, 0:D], meta_w[:, bass.ds(u % RING, 1)],
                                  None, ALU.mult).then_inc(s_y, 1)

            def tile8(buf, t):
                return buf[:, bass.ds(t * E, E)]

            def unit_a(u):
                peeled = isinstance(u, int)
                routes, routed = not peeled or u < UA, not peeled or 1 <= u <= UA
                if routed:
                    dve.wait_ge(s_m8, u)
                if not peeled or u >= 1:
                    low_gT(u - 1, 0)
                if routed:
                    dve.max_index(i8[:, :], m8[:, :], logit[:, :]).then_inc(s_i8, 1)
                if not peeled or u >= 2:
                    shared_y(u - 2, u - 2).then_inc(s_y, 1)
                product(u, 0)
                if routed:
                    own_wait(dve, s_i8, u)
                    dve.tensor_copy(i2f[:, :], i8[:, 0:2])
                    dve.tensor_copy(tile8(m8_all, u - 1), m8[:, :]).then_inc(s_i2f, 1)
                if not peeled or u >= 1:
                    low_gT(u - 1, 1)
                if routed:
                    dve.wait_ge(s_i2f, u)
                    dve.tensor_scalar(tile8(oh1, u - 1), iota8, i2f[:, 0:1], None, ALU.is_equal)
                    dve.tensor_scalar(tile8(oh2, u - 1), iota8, i2f[:, 1:2], None, ALU.is_equal).then_inc(s_oh, 1)
                low_xT(u + 1)
                if routed:
                    dve.wait_ge(s_oh, u)
                    dve.tensor_tensor(tile8(chosen, u - 1), tile8(oh1, u - 1), tile8(oh2, u - 1), ALU.add).then_inc(s_chosen, 1)
                if routes:
                    dve.wait_ge(s_sil[1], u + 1)
                    dve.tensor_copy(logit[:, :], bank[2][:, HALF:HALF + E]).then_inc(s_logit, 1)
                    dve.wait_ge(s_logit, u + 1)
                product(u, 1)
                if routes:
                    dve.max(m8[:, :], logit[:, :]).then_inc(s_m8, 1)
                if routed:
                    dve.wait_ge(s_chosen, u)
                    dve.wait_ge(s_before, u)
                    dve.tensor_tensor(tile8(before, u), tile8(before, u - 1), tile8(chosen, u - 1), ALU.add).then_inc(s_before, 1)

            def unit_b(u):
                low_gT(u - 1, 0)
                shared_y(u - 2, u - 2 - UA).then_inc(s_y, 1)
                product(u, 0)
                low_gT(u - 1, 1)
                low_xT(u + 1)
                product(u, 1)

            def unit_c(u, last=False):
                low_gT(u - 1, 0)
                routed_y(u - 2)
                product(u, 0)
                low_gT(u - 1, 1)
                if not last:
                    low_xT(u + 1)
                product(u, 1)

            chain = [0]

            def step(ins):
                chain[0] += 1
                ins.then_inc(s_r, 1)
                dve.wait_ge(s_r, chain[0])

            def by_tile(buf):
                return buf[:, :].rearrange("p (t e) -> p t e", e=E)

            def over_tiles(buf, n=TILES, parts=P):
                return buf.unsqueeze(1).to_broadcast([parts, n, E])

            def route_1():
                dve.wait_ge(s_rank, 1)
                dve.tensor_copy(pos_e[:, :], bank[6][:, 0:TILES * E])
                dve.tensor_scalar(n_i[:, :], bank[6][:, TILES * E:(TILES + 1) * E], float(P - 1), None,
                                  ALU.add).then_inc(s_rank_read, 1)
                dve.wait_ge(s_rank_read, 1)
                step(dve.tensor_scalar(n_t[:, :], n_i[:, :], 7, None, ALU.arith_shift_right))
                step(dve.tensor_copy(tiles_f[:, :], n_t[:, :]))
                step(dve.tensor_tensor_scan(end_f[:, :], ones8[:, :], tiles_f[:, :], 0.0, ALU.mult, ALU.add))
                step(dve.tensor_tensor(start_f[:, :], end_f[:, :], tiles_f[:, :], ALU.subtract))

            def route_2():
                dve.wait_ge(s_exp, 1)
                step(dve.scalar_tensor_tensor(out=by_tile(pos_e), in0=over_tiles(start_f[:, :]), scalar=float(P),
                                              in1=by_tile(pos_e), op0=ALU.mult, op1=ALU.add))
                for oh, pos_f, pos in ((oh1, pos1f, pos1), (oh2, pos2f, pos2)):
                    step(dve.tensor_tensor(tmp1[:, :], oh[:, :], pos_e[:, :], ALU.mult))
                    step(dve.tensor_reduce(pos_f[:, :], by_tile(tmp1), AX_X, ALU.add))
                    dve.tensor_copy(pos[:, :], pos_f[:, :]).then_inc(s_pos, 1)
                step(dve.memset(ones_s[:, :], 1.0))

            def route_0():
                dve.wait_ge(s_before, UA + 1)
                dve.tensor_tensor(by_tile(tmp1), by_tile(m8_all),
                                  m8_all[:, 0::E].unsqueeze(2).to_broadcast([P, TILES, E]), ALU.subtract).then_inc(s_dlog, 1)

            def route_3():
                step(dve.tensor_reduce(esum[:, :], by_tile(tmp2), AX_X, ALU.add))
                step(dve.reciprocal(esum[:, :], esum[:, :]))
                step(dve.tensor_tensor(w2[:, :], esum[:, :], tmp2[:, 1::E], ALU.mult))
                dve.tensor_tensor(xn2_all[:, W_COL::ROW], esum[:, :], tmp2[:, 0::E], ALU.mult).then_inc(s_w1, 1)

            def route_4():
                iota_s = consts[0:1, IOTA_S:IOTA_S + SLOTS].unsqueeze(2).to_broadcast([1, SLOTS, E])
                ends = over_tiles(end_f[0:1, :], SLOTS, 1)
                a8 = slot8a[:, :].rearrange("p (s e) -> p s e", e=E)
                b8 = slot8b[:, :].rearrange("p (s e) -> p s e", e=E)
                step(dve.tensor_tensor(a8, ends, iota_s, ALU.is_le))
                step(dve.tensor_reduce(e_of[:, 1:], a8, AX_X, ALU.add))
                step(dve.tensor_scalar(e_of[:, 1:], e_of[:, 1:], float(E - 1), None, ALU.min))
                step(dve.scalar_tensor_tensor(out=b8, in0=a8, scalar=1024.0, in1=ends, op0=ALU.mult, op1=ALU.add))
                step(dve.tensor_reduce(end_of[:, :], b8, AX_X, ALU.min))

            def route_5():
                ends = over_tiles(end_f[0:1, :], SLOTS, 1)
                a8 = slot8a[:, :].rearrange("p (s e) -> p s e", e=E)
                step(dve.tensor_tensor(a8, ends, end_of[:, :].unsqueeze(2).to_broadcast([1, SLOTS, E]), ALU.is_le))
                step(dve.tensor_reduce(next_of[:, :], a8, AX_X, ALU.add))
                step(dve.tensor_scalar(next_i[:, :], next_of[:, :], float(E - 1), None, ALU.min))
                step(dve.tensor_copy(e0_i[:, :], e_of[:, 1:2]))
                step(dve.tensor_tensor(first_of[:, :], e_of[:, 1:], e_of[:, 0:SLOTS], ALU.not_equal))
                step(dve.tensor_tensor_scan(run_of[:, 1:], ones_s[:, :], first_of[:, :], 0.0, ALU.mult, ALU.add))

            def route_6():
                step(dve.tensor_copy(run_i[:, :], run_of[:, :]))
                step(dve.tensor_scalar(par_i[:, :], run_i[:, :], 1, None, ALU.bitwise_and))
                step(dve.tensor_scalar(par_i[:, :], par_i[:, :], -1.0, 1.0, ALU.mult, ALU.add))
                step(dve.scalar_tensor_tensor(out=flag_of[:, :], in0=e_of[:, 1:], scalar=float(E - 1), in1=first_of[:, :],
                                              op0=ALU.is_lt, op1=ALU.mult))
                step(dve.scalar_tensor_tensor(out=runs_i[:, :], in0=run_of[:, 0:SLOTS], scalar=16.0, in1=run_of[:, 1:],
                                              op0=ALU.mult, op1=ALU.add))
                step(dve.tensor_copy(flag_i[:, :], flag_of[:, :]))
                step(dve.tensor_tensor(fetch_i[0][:, :], flag_i[:, :], par_i[:, 1:], ALU.mult))
                dve.tensor_tensor(fetch_i[1][:, :], flag_i[:, :], fetch_i[0][:, :], ALU.subtract).then_inc(s_tables, 1)

            def route_7():
                dve.wait_ge(s_sort1, 16 * TILES)
                dve.tensor_copy(xn2_all[:, W_COL::ROW], w2[:, :]).then_inc(s_w2, 1)

            dve.wait_ge(s_acc, TILES)
            dve.memset(tile8(before, 0), 0.0).then_inc(s_before, 1)
            dve.memset(ones8[:, :], 1.0)
            dve.memset(e_of[:, 0:1], -1.0)
            dve.memset(run_of[:, 0:1], 0.0)
            for u in range(3):
                unit_a(u)
            with dve.Fori(3, UA) as u:
                unit_a(u)
            unit_a(UA)
            route_0()
            unit_a(UA + 1)
            routing = [route_1, route_2, route_3, route_4, route_5, route_6]
            for k, stage in enumerate(routing):
                stage()
                unit_b(UA + 2 + k)
            with dve.Fori(UA + 2 + len(routing), UB - 15) as u:
                unit_b(u)
            route_7()
            with dve.Fori(UB - 15, UB) as u:
                unit_b(u)
            unit_b(UB)
            unit_b(UB + 1)
            for u in range(UB + 2, UB + 2 + RING):
                unit_c(u)
            with dve.Fori(UB + 2 + RING, UNITS - 1) as u:
                unit_c(u)
            unit_c(UNITS - 1, last=True)
            low_gT(UNITS - 1, 0)
            routed_y(UNITS - 2)
            low_gT(UNITS - 1, 1)
            routed_y(UNITS - 1)

        @block.tensor
        def _(pe):
            def transposes(dst, src, n):
                for c in range(n):
                    mm = pe.transpose(dst[:, c * P:(c + 1) * P], src[:, c * P:(c + 1) * P], ident)
                return mm

            def support(t, b):
                peeled = isinstance(t, int)
                if not peeled or t < TILES:
                    pe.wait_ge(s_xc, t + 1)
                    at_least(pe, s_xcl, t - 1)
                    transposes(bank[b], xc[b], DC).then_inc(s_xT1, 1)
                if not peeled or t >= 1:
                    pe.wait_ge(s_xcl, t)
                    if peeled and t == 1:
                        pe.wait_ge(s_wg, 2)
                    at_least(pe, s_sl, t - 2)
                    k = 0
                    for c in range(DC):
                        high, low = xcT_h[1 - b][:, c * P:(c + 1) * P], xcT_l[1 - b][:, c * P:(c + 1) * P]
                        wh, wl = w_gnn_h[:, c * D:(c + 1) * D], w_gnn_l[:, c * D:(c + 1) * D]
                        for lhs, rhs in ((high, wh), (high, wl), (low, wh)):
                            mm = pe.matmul(bank[3 - b][:, 0:D], lhs, rhs, start=(k == 0), stop=(k == 3 * DC - 1))
                            k += 1
                    mm.then_inc(s_smm, 1)

            def loop(first, end):
                return nc.Fori(first, end, engines=(mybir.EngineType.PE,), hint_back_edge=True)

            pe.wait_ge(s_cst, 16)
            for t in range(4):
                support(t, t % 2)
            with loop(2, TILES // 2) as pair:
                support(2 * pair, 0)
                support(2 * pair + 1, 1)
            support(TILES, 0)

            def row_block(t, acc):
                at_least(pe, s_x1, t - 1)
                for h in range(2):
                    pe.wait_ge(s_al, 2 * t + h + 1)
                    for k in range(HALF_J):
                        j = h * HALF_J + k
                        high, low = adj_h[h][:, k * P:(k + 1) * P], adj_l[h][:, k * P:(k + 1) * P]
                        pe.matmul(acc[:, 0:2 * D], high, s_hl[:, j * 2 * D:(j + 1) * 2 * D], start=(j == 0), stop=False)
                        mm = pe.matmul(acc[:, D:2 * D], low, s_hl[:, j * 2 * D:j * 2 * D + D], start=False,
                                       stop=(j == TILES - 1))
                    mm.then_inc(s_half[h], 1)

            pe.wait_ge(s_sl, TILES)
            row_block(0, bank[4])
            row_block(1, bank[5])
            with loop(1, TILES // 2 - 1) as pair:
                row_block(2 * pair, bank[4])
                row_block(2 * pair + 1, bank[5])
            row_block(TILES - 2, bank[4])
            pe.wait_ge(s_xt, 16)
            transposes(bank[6], xt, DC).then_inc(s_xT, 1)
            row_block(TILES - 1, bank[5])

            def w_part(buffer, low, part):
                def at(col, n):
                    return W[:, bass.ds(buffer * (2 * WCOLS) + (low * WCOLS + PART_AT[part] + col), n)]
                return at

            def xT_of(u):
                pe.wait_ge(s_xt, 16 * u + 16)
                at_least(pe, s_xTl, u)
                transposes(bank[6], xt, DC).then_inc(s_xT, 1)

            def up(u, h, buffer, gate_too=False):
                pe.wait_ge(s_xTl, u + 1)
                at_least(pe, s_g[h], u)
                for part, dst in ((0, bank[2 * h]), (1, bank[2 * h + 1])):
                    k = 0
                    n = HALF + (E if gate_too and part == 0 else 0)
                    for c in range(DC):
                        high, low = xT_h[:, c * P:(c + 1) * P], xT_l[:, c * P:(c + 1) * P]
                        col = c * (PARTS[part] // DC) + h * HALF
                        for a, b in ((high, 0), (high, 1), (low, 0)):
                            mm = pe.matmul(dst[:, 0:n], a, w_part(buffer, b, part)(col, n), start=(k == 0),
                                           stop=(k == 3 * DC - 1))
                            k += 1
                mm.then_inc(s_up[h], 1)

            def turn(u, h):
                pe.wait_ge(s_g[h], u + 1)
                at_least(pe, s_gTl[h], u)
                transposes(bank[4 + h], g[h], HC // 2).then_inc(s_gT[h], 1)

            def down(u, h, buffer):
                pe.wait_ge(s_gTl[h], u + 1)
                if h == 0:
                    at_least(pe, s_y, u)
                for k in range(HC // 2):
                    high, low = gT_h[h][:, k * P:(k + 1) * P], gT_l[h][:, k * P:(k + 1) * P]
                    col = (h * (HC // 2) + k) * D
                    for n, (a, b) in enumerate(((high, 0), (high, 1), (low, 0))):
                        mm = pe.matmul(bank[7][:, 0:D], a, w_part(buffer, b, 2)(col, D), start=(h == 0 and k == 0 and n == 0),
                                       stop=(h == 1 and k == HC // 2 - 1 and n == 2))
                if h == 1:
                    mm.then_inc(s_down, 1)

            def ranks():
                pe.wait_ge(s_before, UA + 1)
                pe.matmul(bank[6][:, 0:TILES * E], tri, chosen[:, :], start=True, stop=False, skip_group_check=True)
                pe.matmul(bank[6][:, 0:TILES * E], ones_pp, before[:, 0:TILES * E], start=False, stop=True, skip_group_check=True)
                pe.matmul(bank[6][:, TILES * E:(TILES + 1) * E], ones_pp, before[:, TILES * E:(TILES + 1) * E], start=False,
                          stop=True, skip_group_check=True).then_inc(s_rank, 1)

            def unit(u, buffer, buffer_before, gate_too=False, last=False, rank=False, whole=None, whole_before=None):
                first = isinstance(u, int) and u == 0
                if whole is not None:
                    pe.wait_ge(s_wl, whole - 1)
                up(u, 0, buffer)
                if not first:
                    turn(u - 1, 1)
                if rank:
                    ranks()
                    pe.wait_ge(s_rank_read, 1)
                if not last:
                    xT_of(u + 1)
                up(u, 1, buffer, gate_too)
                if not first:
                    if whole_before is not None:
                        pe.wait_ge(s_wl, whole_before)
                    down(u - 1, 0, buffer_before)
                turn(u, 0)
                if not first:
                    down(u - 1, 1, buffer_before)

            unit(0, 0, 0, gate_too=True, whole=3)
            unit(1, 0, 0, gate_too=True, whole_before=3)
            with loop(2, UA) as u:
                unit(u, 0, 0, gate_too=True)
            unit(UA, 1, 0, whole=6)
            unit(UA + 1, 1, 1, whole_before=6)
            unit(UA + 2, 1, 1, rank=True)
            with loop(UA + 3, UB) as u:
                unit(u, 1, 1)
            pe.wait_ge(s_tables, 1)

            def routed(s, last=False):
                both = pe.value_load(runs_i[0:1, bass.ds(s, 1)], min_val=1, max_val=16 * E + E)
                run, run_before = both % 16, both // 16
                par, par_before = (run + 1) % 2, (run_before + 1) % 2
                unit(s + UB, par, par_before, whole=run * 3 + 6, whole_before=run_before * 3 + 6, last=last)

            with loop(0, SLOTS - 1) as s:
                routed(s)
            routed(SLOTS - 1, last=True)
            par = pe.value_load(par_i[0:1, SLOTS:SLOTS + 1], min_val=0, max_val=1)
            turn(UNITS - 1, 1)
            down(UNITS - 1, 0, par)
            down(UNITS - 1, 1, par)


def kernel(x, adj, L0_gnn_weight, L0_gnn_bias, L0_ffn_gate_w, L0_ffn_w1, L0_ffn_w3, L0_ffn_w2,
           L0_ffn_sw1, L0_ffn_sw3, L0_ffn_sw2):
    import concourse.bacc as bacc
    from concourse.bass_utils import run_bass_kernel_spmd

    def np32(a):
        return np.asarray(a, dtype=np.float32)

    def features_on_partitions(w):
        return np.ascontiguousarray(w.T.reshape(DC, P, -1).transpose(1, 0, 2)).reshape(P, -1)

    x, adj = np32(x), np32(adj)
    pad = NP - N
    x_in = np.pad(x, ((0, pad), (0, 0))).reshape(TILES, P, D).transpose(1, 0, 2).reshape(P, TILES * D)
    adj_p = np.pad(adj, ((0, pad), (0, pad))).reshape(TILES, P, TILES, P)
    adj_in = np.ascontiguousarray(adj_p.transpose(0, 3, 2, 1)).reshape(TILES * P, TILES * P)
    w_in = np32(L0_gnn_weight).reshape(DC, P, D).transpose(1, 0, 2).reshape(P, DC * D)
    bias_in = np.tile(np32(L0_gnn_bias)[None, :], (P, 1))
    gate = np32(L0_ffn_gate_w)
    sw1, sw3, sw2 = np32(L0_ffn_sw1), np32(L0_ffn_sw3), np32(L0_ffn_sw2)
    w1 = list(sw1.reshape(2, HID, D)) + list(np32(L0_ffn_w1))
    w3 = list(sw3.reshape(2, HID, D)) + list(np32(L0_ffn_w3))
    w2 = [sw2[:, :HID], sw2[:, HID:]] + list(np32(L0_ffn_w2))
    down = [np.ascontiguousarray(w.T.reshape(HC, P, D).transpose(1, 0, 2)).reshape(P, -1) for w in w2]
    w1 = [np.concatenate([w, gate if n == 0 else np.zeros_like(gate)]) for n, w in enumerate(w1)]
    experts_in = np.concatenate([np.concatenate([features_on_partitions(a), features_on_partitions(b), c], axis=1)
                                 for a, b, c in zip(w1, w3, down)])
    cst = np.zeros((P, CST), np.float32)
    cst[:, IDENT:IDENT + P] = np.eye(P)
    cst[:, TRI:TRI + P] = np.triu(np.ones((P, P)), 1)
    cst[:, IOTA8:IOTA8 + E] = np.arange(E)
    cst[:, ONES:ONES + P] = 1
    cst[:, IOTA_S:IOTA_S + SLOTS] = np.arange(SLOTS)

    nc = bacc.Bacc("TRN2", target_bir_lowering=False, num_devices=1)
    arrays = {"x_in": x_in, "adj_in": adj_in, "w_in": w_in, "bias_in": bias_in,
              "experts_in": experts_in, "cst_in": cst}
    arrays = {k: np.ascontiguousarray(v) for k, v in arrays.items()}
    args = [nc.dram_tensor(k, list(v.shape), F32, kind="ExternalInput").ap() for k, v in arrays.items()]
    out = nc.dram_tensor("out", [NP + P, D], F32, kind="ExternalOutput").ap()
    build(nc, *args, out)
    r = run_bass_kernel_spmd(nc, [arrays], core_ids=[0])
    return r.results[0]["out"][:N]
```

```python
from contextlib import ExitStack

import numpy as np

import concourse.bass as bass
from concourse import mybir

F32 = mybir.dt.float32
F32R = mybir.dt.float32r
I32 = mybir.dt.int32
U32 = mybir.dt.uint32
ALU = mybir.AluOpType
ACT = mybir.ActivationFunctionType
AX_X = mybir.AxisListType.X

P = 128
N = 3327
D = 256
DC = D // P
E = 8
HID = 768
HC = HID // P
HALF = HID // 2
TILES = -(-N // P)
NP = TILES * P
HALF_J = TILES // 2
CHUNK = 4
WIDE = CHUNK * P
CHUNKS = -(-TILES // CHUNK)
LAST = CHUNKS - 1
SLOTS = (2 * NP) // P + E - 1
SURE = SLOTS - (E - 1)
ROW = D + 4
ID_COL, W_COL = D, D + 1
W1_COLS = HID + E
PARTS = (DC * W1_COLS, DC * HID, HC * D)
PART_AT = (0, PARTS[0], PARTS[0] + PARTS[1])
WCOLS = sum(PARTS)
X_PIECES = [0, 2, 4, 10, 18]
SPLIT_AT = [8, 16]
BEHIND = 10
TURN = 3
RING = 4
EPS = 1e-5
IDENT, TRI, ONES, IOTA8, IOTA_S = 0, P, 2 * P, 3 * P, 3 * P + E
CST = IOTA_S + SLOTS


def at_least(eng, sem, value):
    if isinstance(value, int) and value <= 0:
        return
    eng.wait_ge(sem, value)


def tiles_in(q):
    return TILES - LAST * CHUNK if q % CHUNKS == LAST else CHUNK


def build(nc, x, adj, w_gnn, bias, weights, cst, out):
    xn_dram = nc.dram_tensor("xn_dram", [NP, ROW], F32, kind="Internal").ap()
    sorted_dram = nc.dram_tensor("sorted_dram", [SLOTS * P, ROW], F32, kind="Internal").ap()

    place = [-(-nc.sbuf_base // 32) * 32]

    def sb(name, cols, dt=F32, parts=P):
        t = nc.alloc_sbuf_tensor_at(name, [parts, cols], dt, offset=place[0])
        place[0] += -(-cols * 4 // 32) * 32
        return t

    ctx = ExitStack()
    with ctx:
        x_all = sb("x_all", TILES * D)
        xn2_all = sb("xn2_all", TILES * ROW)
        raw_w = sb("raw_w", WCOLS)
        consts = sb("consts", CST)
        small = sb("small", 32)
        mv_all = sb("mv_all", 2 * TILES)
        sd_all = sb("sd_all", TILES)
        rs_all = sb("rs_all", TILES)
        zrow = sb("zrow", ROW)
        meta_id = sb("meta_id", RING, I32)
        meta_w = sb("meta_w", RING)
        rows_in = sb("rows_in", CHUNK * ROW)
        w_start = place[0]
        W = nc.alloc_sbuf_tensor_at("W", [P, 2 * 2 * WCOLS], F32R, offset=w_start)
        first_layer = w_start + 2 * WCOLS * 4
        place[0] = first_layer
        s_hl = sb("s_hl", TILES * 2 * D, F32R)
        adj_raw, adj_l = [[None, None], [None, None]], [[None, None], [None, None]]

        def neighbours_at(b, h):
            adj_raw[b][h] = nc.alloc_sbuf_tensor_at(f"adj_raw{b}{h}", [P, HALF_J * P], F32, offset=place[0])
            adj_l[b][h] = sb(f"adj_l{b}{h}", HALF_J * P, F32R)

        neighbours_at(0, 1)
        neighbours_at(1, 1)
        free_early = place[0]
        neighbours_at(0, 0)
        adj_h = [sb("adj_h0", HALF_J * P, F32R)]
        neighbours_at(1, 0)
        adj_h.append(sb("adj_h1", HALF_J * P, F32R))
        bias_sb = sb("bias_sb", D)
        assert place[0] <= nc.sbuf_usable_end, (place[0], nc.sbuf_usable_end)
        place[0] = w_start
        w_gnn_raw = sb("w_gnn_raw", DC * D)
        w_gnn_h = sb("w_gnn_h", DC * D, F32R)
        w_gnn_l = sb("w_gnn_l", DC * D, F32R)
        xc = [sb(f"xc{b}", D) for b in range(2)]
        xcT_h = [sb(f"xcT_h{b}", D, F32R) for b in range(2)]
        xcT_l = [sb(f"xcT_l{b}", D, F32R) for b in range(2)]
        assert place[0] <= first_layer
        place[0] = first_layer + 2 * WCOLS * 4
        sil = [sb(f"sil{b}", WIDE) for b in range(2)]
        g = [sb(f"g{b}", WIDE) for b in range(2)]
        gT_h = [sb(f"gT_h{b}", WIDE, F32R) for b in range(2)]
        gT_l = [sb(f"gT_l{b}", WIDE, F32R) for b in range(2)]
        y_ring = sb("y_ring", RING * D)
        xTc_h, xTc_l = [None, sb("xTc_h1", DC * WIDE, F32R)], [None, sb("xTc_l1", DC * WIDE, F32R)]
        assert place[0] <= free_early
        place[0] = free_early
        xTc_h[0], xTc_l[0] = sb("xTc_h0", DC * WIDE, F32R), sb("xTc_l0", DC * WIDE, F32R)
        xt = sb("xt", ROW)
        xT_h = sb("xT_h", D, F32R)
        xT_l = sb("xT_l", D, F32R)
        id_ring = sb("id_ring", RING, I32)
        gate_hl = sb("gate_hl", DC * 2 * E, F32R)
        logit_l = sb("logit_l", CHUNK * E)
        logit = sb("logit", CHUNK * E)
        m8 = sb("m8", CHUNK * E)
        i8 = sb("i8", CHUNK * E, U32)
        i2f = [sb(f"i{n}f", CHUNK) for n in (1, 2)]
        m8_all = sb("m8_all", TILES * E)
        oh1 = sb("oh1", TILES * E)
        oh2 = sb("oh2", TILES * E)
        chosen = sb("chosen", TILES * E)
        before = sb("before", (TILES + 1) * E)
        pos_e = sb("pos_e", TILES * E)
        tmp1 = sb("tmp1", TILES * E)
        tmp2 = sb("tmp2", TILES * E)
        esum = sb("esum", TILES)
        w2 = sb("w2", TILES)
        pos1f = sb("pos1f", TILES)
        pos2f = sb("pos2f", TILES)
        pos1 = sb("pos1", TILES, I32)
        pos2 = sb("pos2", TILES, I32)
        n_i = sb("n_i", E, I32)
        n_t = sb("n_t", E, I32)
        tiles_f = sb("tiles_f", E)
        ones8 = sb("ones8", E)
        end_f = sb("end_f", E)
        start_f = sb("start_f", E)
        slot8a = sb("slot8a", SLOTS * E, parts=1)
        slot8b = sb("slot8b", SLOTS * E, parts=1)
        e_of = sb("e_of", SLOTS + 1, parts=1)
        end_of = sb("end_of", SLOTS, parts=1)
        next_of = sb("next_of", SLOTS, parts=1)
        first_of = sb("first_of", SLOTS, parts=1)
        ones_s = sb("ones_s", SLOTS, parts=1)
        run_of = sb("run_of", SLOTS + 1, parts=1)
        flag_of = sb("flag_of", SLOTS, parts=1)
        run_i = sb("run_i", SLOTS + 1, I32, parts=1)
        par_i = sb("par_i", SLOTS + 1, I32, parts=1)
        runs_i = sb("runs_i", SLOTS, I32, parts=1)
        flag_i = sb("flag_i", SLOTS, I32, parts=1)
        fetch_i = [sb(f"fetch_i{b}", SLOTS, I32, parts=1) for b in range(2)]
        next_i = sb("next_i", SLOTS, I32, parts=1)
        e0_i = sb("e0_i", 1, I32, parts=1)
        more_i = sb("more_i", 1, I32, parts=1)
        assert place[0] <= nc.sbuf_usable_end
        bank = [ctx.enter_context(nc.psum_tensor(f"bank{b}", [P, 512], F32)) for b in range(8)]

        st = [small[:, 0:6], small[:, 26:32]]
        eps = small[:, 10:11]
        st2, mv2, sd2, rs2 = small[:, 16:22], small[:, 22:24], small[:, 24:25], small[:, 25:26]
        ident = consts[:, IDENT:IDENT + P]
        tri = consts[:, TRI:TRI + P]
        ones_pp = consts[:, ONES:ONES + P]
        iota8 = consts[:, IOTA8:IOTA8 + E]

        def sem(name):
            return ctx.enter_context(nc.semaphore(name))

        s_x_in = [sem(f"s_x_in{i}") for i in range(len(X_PIECES))]
        s_w_gnn_in = sem("s_w_gnn_in")
        s_consts_in = sem("s_consts_in")
        s_bias_in = sem("s_bias_in")
        s_adj_in = [[sem(f"s_adj_in{b}{h}") for h in range(2)] for b in range(2)]
        s_weights_in = [sem(f"s_weights_in{i}") for i in range(3)]
        s_sorted_emptied = sem("s_sorted_emptied")
        s_trash_rows = sem("s_trash_rows")
        s_rows_out = sem("s_rows_out")
        s_unit_in = sem("s_unit_in")
        s_sorted1 = sem("s_sorted1")
        s_sorted2 = sem("s_sorted2")
        s_shared_out = sem("s_shared_out")
        s_added = sem("s_added")
        s_passed = sem("s_passed")
        s_eps = sem("s_eps")
        s_empty_zero = sem("s_empty_zero")
        s_empty_number = sem("s_empty_number")
        s_w_gnn_split = sem("s_w_gnn_split")
        s_numbers = sem("s_numbers")
        s_rows_zero = sem("s_rows_zero")
        s_bn_stats = sem("s_bn_stats")
        s_mean_var = sem("s_mean_var")
        s_deviation = sem("s_deviation")
        s_inverse = sem("s_inverse")
        s_centred = sem("s_centred")
        s_centred_turned = sem("s_centred_turned")
        s_centred_high = sem("s_centred_high")
        s_centred_low = sem("s_centred_low")
        s_support = sem("s_support")
        s_support_high = sem("s_support_high")
        s_support_low = sem("s_support_low")
        s_x_biased = sem("s_x_biased")
        s_adj_high = sem("s_adj_high")
        s_adj_low = sem("s_adj_low")
        s_half_summed = [sem("s_half0"), sem("s_half1")]
        s_row_block_summed = s_half_summed[1]
        s_x1_part = sem("s_x1_part")
        s_x1 = sem("s_x1")
        s_bn_stats2 = sem("s_bn_stats2")
        s_mean_var2 = sem("s_mean_var2")
        s_deviation2 = sem("s_deviation2")
        s_inverse2 = sem("s_inverse2")
        s_x1_normed = sem("s_x1_normed")
        s_weights_high = sem("s_weights_high")
        s_weights_low = sem("s_weights_low")
        s_unit_turned = sem("s_unit_turned")
        s_unit_high = sem("s_unit_high")
        s_unit_low = sem("s_unit_low")
        s_meta = sem("s_meta")
        s_up = [sem("s_up0"), sem("s_up1")]
        s_silu = [sem("s_sil0"), sem("s_sil1")]
        s_product = [sem("s_g0"), sem("s_g1")]
        s_product_turned = [sem("s_gT0"), sem("s_gT1")]
        s_product_high = [sem("s_gTh0"), sem("s_gTh1")]
        s_product_low = [sem("s_gTl0"), sem("s_gTl1")]
        s_down = sem("s_down")
        s_y_taken = sem("s_y_taken")
        s_chunk_in = sem("s_chunk_in")
        s_chunk_turned = sem("s_chunk_turned")
        s_chunk_high = sem("s_chunk_high")
        s_chunk_low = sem("s_chunk_low")
        s_chunk_up = sem("s_chunk_up")
        s_chunk_silu = sem("s_chunk_silu")
        s_chunk_product = sem("s_chunk_product")
        s_chunk_product_high = sem("s_chunk_product_high")
        s_chunk_product_low = sem("s_chunk_product_low")
        s_chunk_down = sem("s_chunk_down")
        s_chunk_added = sem("s_chunk_added")
        s_gate = sem("s_gate")
        s_logit_parts = sem("s_logit_parts")
        s_logit_low = sem("s_logit_low")
        s_logit = sem("s_logit")
        s_best8 = sem("s_best8")
        s_best8_number = sem("s_best8_number")
        s_best2_number = sem("s_best2_number")
        s_one_hot = sem("s_one_hot")
        s_chosen = sem("s_chosen")
        s_before = sem("s_before")
        s_ranks = sem("s_ranks")
        s_ranks_read = sem("s_ranks_read")
        s_logit_less_max = sem("s_logit_less_max")
        s_exp = sem("s_exp")
        s_routing_step = sem("s_routing_step")
        s_places = sem("s_places")
        s_weight1 = sem("s_weight1")
        s_weight2 = sem("s_weight2")
        s_tables = sem("s_tables")
        s_first_expert = sem("s_first_expert")

        block = ctx.enter_context(nc.Block())

        def own_wait(eng, sem, value):
            at_least(eng, sem, value)
            if not isinstance(value, int):
                eng.sem_inc(s_passed, 1)

        def rows(t):
            return bass.ds(t * P, P)

        def xtile(t):
            return x_all[:, bass.ds(t * D, D)]

        def load_part(eng, e, n, part):
            at_least(eng, s_weights_low, 3 * (n - 1) + part + 1)
            at, cols = PART_AT[part], PARTS[part]
            eng.dma_start(raw_w[:, at:at + cols], weights[rows(e), at:at + cols]).then_inc(s_weights_in[part], 16)

        def load_expert(eng, e, n):
            for part in range(3):
                load_part(eng, e, n, part)

        def units_more(eng):
            eng.wait_ge(s_tables, 1)
            return eng.value_load(more_i[0:1, 0:1], min_val=0, max_val=SLOTS - SURE)

        def in_chunks(loop, chunk):
            for half in range(2):
                first = half * CHUNKS

                def one(q):
                    chunk(q, q % 2, half, tiles_in(q), tiles_in(q + 1) if q + 1 < 2 * CHUNKS else 0)

                one(first)
                with loop(0, (CHUNKS - 3) // 2) as pair:
                    for k in (1, 2):
                        chunk(2 * pair + (first + k), (first + k) % 2, half, CHUNK, CHUNK)
                one(first + CHUNKS - 2)
                one(first + CHUNKS - 1)

        @block.sync
        def _(sp):
            sp.dma_start(x_all[:, 0:2 * D], x[:, 0:2 * D]).then_inc(s_x_in[0], 16)
            sp.dma_start(w_gnn_raw[:, :], w_gnn).then_inc(s_w_gnn_in, 16)
            sp.dma_start(consts[:, :], cst).then_inc(s_consts_in, 16)
            for piece in range(1, len(X_PIECES)):
                part = slice(X_PIECES[piece] * D, (X_PIECES + [TILES])[piece + 1] * D)
                sp.dma_start(x_all[:, part], x[:, part]).then_inc(s_x_in[piece], 16)
            sp.dma_start(bias_sb[:, :], bias).then_inc(s_bias_in, 16)

            def adj_load(t, b, h):
                own_wait(sp, s_half_summed[h], t - 1)
                sp.dma_start(adj_raw[b][h][:, :], adj[rows(t), h * HALF_J * P:(h + 1) * HALF_J * P]
                    ).then_inc(s_adj_in[b][h], 16)

            def xn_store(t):
                own_wait(sp, s_x1_normed, t + 1)
                own_wait(sp, s_rows_out, 16 * t)
                sp.dma_start(xn_dram[rows(t), :], xn2_all[:, bass.ds(t * ROW, ROW)]).then_inc(s_rows_out, 16)

            def chunk_load(q, n=CHUNK):
                at_least(sp, s_chunk_turned, q)
                source = xn_dram[bass.ds(q % CHUNKS * WIDE, n * P), :].rearrange("(t p) d -> p t d", p=P)
                sp.dma_start(rows_in[:, 0:n * ROW].rearrange("p (t d) -> p t d", d=ROW), source).then_inc(s_chunk_in, 16)

            def out_store(q):
                sp.wait_ge(s_chunk_added, q + 1)
                for k in range(tiles_in(q)):
                    t = (q - CHUNKS) * CHUNK + k
                    sp.dma_start(out[rows(t), :], xtile(t)).then_inc(s_shared_out, 16)

            def unit_load(s):
                at_least(sp, s_unit_turned, s)
                at_least(sp, s_meta, s)
                sp.dma_start(xt[:, :], sorted_dram[rows(s), :]).then_inc(s_unit_in, 16)

            for t in range(2):
                for h in range(2):
                    adj_load(t, t, h)
                if t == 0:
                    load_expert(sp, 0, 0)
            sp.wait_ge(s_numbers, TILES)
            sp.wait_ge(s_rows_zero, 1)
            for t in (2, 3):
                adj_load(t, t % 2, 0)
                adj_load(t, t % 2, 1)
            xn_store(0)
            with sp.Fori(2, TILES // 2) as pair:
                for b in range(2):
                    adj_load(2 * pair + b, b, 0)
                    adj_load(2 * pair + b, b, 1)
                    xn_store(2 * pair + (b - 3))
            xn_store(TILES - 3)
            chunk_load(0)
            xn_store(TILES - 2)
            chunk_load(1)
            xn_store(TILES - 1)
            sp.wait_ge(s_rows_out, 16 * TILES)
            for part in range(3):
                load_part(sp, 1, 1, part)
            for q in range(2, CHUNKS + 2):
                chunk_load(q, tiles_in(q))
            sp.wait_ge(s_first_expert, 1)
            e0 = sp.value_load(e0_i[0:1, 0:1], min_val=0, max_val=E - 1)
            for q in range(CHUNKS + 2, 2 * CHUNKS):
                if q - (CHUNKS + 2) < 3:
                    load_part(sp, e0 + 2, 2, q - (CHUNKS + 2))
                chunk_load(q, tiles_in(q))
                out_store(q - 2)

            def fetch(s, part):
                flag = sp.value_load(flag_i[0:1, bass.ds(s, 1)], min_val=0, max_val=1)
                with sp.If(flag > 0):
                    e = sp.value_load(next_i[0:1, bass.ds(s, 1)], min_val=0, max_val=E - 1)
                    run1 = sp.value_load(run_i[0:1, bass.ds(s + 1, 1)], min_val=1, max_val=E)
                    load_part(sp, e + 2, run1 + 2, part)

            sp.wait_ge(s_sorted1, 16 * TILES)
            sp.wait_ge(s_sorted2, 16 * TILES)
            unit_load(0)
            more = units_more(sp)
            fetch(0, 0)
            out_store(2 * CHUNKS - 2)
            for s in (1, 2):
                unit_load(s)
                for part in reversed(range(s + 1)):
                    fetch(s - part, part)
            out_store(2 * CHUNKS - 1)
            with sp.Fori(3, SURE + 1) as s:
                unit_load(s)
                for part in reversed(range(3)):
                    fetch(s - part, part)
            with sp.Fori(SURE + 1, SLOTS) as s:
                with sp.If(more + (SURE + 1) > s):
                    unit_load(s)
                for part in reversed(range(3)):
                    fetch(s - part, part)
            for s in range(SLOTS, SLOTS + 2):
                for part in reversed(range(s - SLOTS + 1, 3)):
                    fetch(s - part, part)

        @block.gpsimd
        def _(pool):
            for t in range(TILES):
                at_least(pool, s_centred_turned, t - 1)
                pool.wait_ge(s_mean_var, t + 1)
                pool.tensor_tensor(xc[t % 2][:, :], xtile(t), mv_all[:, 2 * t:2 * t + 1].to_broadcast([P, D]),
                                   ALU.subtract).then_inc(s_centred, 1)
            pool.memset(zrow[:, :], 0.0).then_inc(s_empty_zero, 1)
            pool.memset(xn2_all[:, :], 0.0).then_inc(s_rows_zero, 1)
            pool.wait_ge(s_empty_zero, 1)
            pool.iota(zrow[:, ID_COL:ID_COL + 1].bitcast(I32), [[0, 1]], base=NP, channel_multiplier=1
                ).then_inc(s_empty_number, 1)
            pool.wait_ge(s_empty_number, 1)
            pool.wait_ge(s_rows_zero, 1)
            for t in range(TILES):
                pool.iota(xn2_all[:, t * ROW + ID_COL:t * ROW + ID_COL + 1].bitcast(I32), [[0, 1]], base=t * P,
                          channel_multiplier=1).then_inc(s_numbers, 1)
            pool.wait_ge(s_bias_in, 16)
            pool.wait_ge(s_centred, TILES)
            with pool.Fori(0, TILES) as t:
                pool.tensor_tensor(xtile(t), xtile(t), bias_sb[:, :], ALU.add).then_inc(s_x_biased, 1)
            pool.dma_start(out[rows(TILES), :], zrow[:, 0:D]).then_inc(s_trash_rows, 16)
            with pool.Fori(0, SLOTS) as s:
                pool.dma_start(sorted_dram[rows(s), :], zrow[:, :]).then_inc(s_sorted_emptied, 16)

            def split_expert(n, buffer):
                for part in range(3):
                    at, cols = PART_AT[part], PARTS[part]
                    high = W[:, buffer * 2 * WCOLS + at:buffer * 2 * WCOLS + at + cols]
                    low = W[:, (buffer * 2 + 1) * WCOLS + at:(buffer * 2 + 1) * WCOLS + at + cols]
                    raw = raw_w[:, at:at + cols]
                    own_wait(pool, s_weights_in[part], 16 * (n + 1))
                    pool.tensor_scalar(high, raw, 1.0, 1.0, ALU.mult, ALU.mult).then_inc(s_weights_high, 1)
                    pool.wait_ge(s_weights_high, 3 * n + part + 1)
                    pool.tensor_tensor(low, raw, high.bitcast(F32), ALU.subtract).then_inc(s_weights_low, 1)

            pool.wait_ge(s_support_low, TILES)
            split_expert(0, 0)
            pool.wait_ge(s_row_block_summed, TILES)
            split_expert(1, 1)
            def sort(pos, done):
                pool.wait_ge(s_places, 2)
                for t in range(TILES):
                    pool.indirect_dma_start(sorted_dram[:, :], bass.IndirectOffsetOnAxis(ap=pos[:, t:t + 1], axis=0),
                                            xn2_all[:, t * ROW:(t + 1) * ROW], None).then_inc(done, 16)

            pool.wait_ge(s_sorted_emptied, 16 * SLOTS)
            pool.wait_ge(s_weight1, 1)
            sort(pos1, s_sorted1)
            pool.wait_ge(s_chunk_down, CHUNKS * HC)
            split_expert(2, 0)
            pool.wait_ge(s_sorted1, 16 * TILES)
            pool.tensor_copy(xn2_all[:, W_COL::ROW], w2[:, :]).then_inc(s_weight2, 1)
            pool.wait_ge(s_weight2, 1)
            sort(pos2, s_sorted2)
            pool.wait_ge(s_shared_out, 16 * TILES)
            pool.wait_ge(s_trash_rows, 16)

            def routed_unit(s, slot):
                for buffer in range(2):
                    flag = pool.value_load(fetch_i[buffer][0:1, bass.ds(s, 1)], min_val=0, max_val=1)
                    with pool.If(flag > 0):
                        run1 = pool.value_load(run_i[0:1, bass.ds(s + 1, 1)], min_val=1, max_val=E)
                        if isinstance(s, int) and s == 0:
                            pool.wait_ge(s_chunk_down, 2 * CHUNKS * HC)
                        else:
                            own_wait(pool, s_down, s)
                        split_expert(run1 + 2, buffer)
                own_wait(pool, s_y_taken, s + 1)
                if not isinstance(s, int) or s > 0:
                    own_wait(pool, s_added, s * 16)
                pool.indirect_dma_start(out[:, :], bass.IndirectOffsetOnAxis(ap=id_ring[:, slot:slot + 1], axis=0),
                                        y_ring[:, slot * D:(slot + 1) * D], None, compute_op=ALU.add).then_inc(s_added, 16)

            for s in range(RING):
                routed_unit(s, s)
            assert SURE % RING == 0
            with pool.Fori(1, SURE // RING) as q:
                for slot in range(RING):
                    routed_unit(q * RING + slot, slot)
            more = units_more(pool)
            for s in range(SURE, SLOTS):
                with pool.If(more + SURE > s):
                    routed_unit(s, s % RING)
            pool.wait_ge(s_added, more * 16 + SURE * 16)

        @block.scalar
        def _(act):
            def support(t):
                if t + 3 < TILES:
                    act.wait_ge(s_mean_var, t + 4)
                    act.activation(sd_all[:, t + 3:t + 4], mv_all[:, 2 * (t + 3) + 1:2 * (t + 3) + 2], ACT.Sqrt,
                                   bias=eps).then_inc(s_deviation, 1)
                if t >= 0:
                    act.wait_ge(s_inverse, t + 1)
                    act.wait_ge(s_support, t + 1)
                    act.activation(s_hl[:, t * (2 * D):t * (2 * D) + D], bank[2 + t % 2][:, 0:D], ACT.Copy,
                                   scale=rs_all[:, t:t + 1]).then_inc(s_support_high, 1)
                if -2 <= t < TILES - 2:
                    at_least(act, s_centred_low, t + 1)
                    act.wait_ge(s_centred_turned, t + 3)
                    act.activation(xcT_h[t % 2][:, :], bank[t % 2][:, 0:D], ACT.Copy).then_inc(s_centred_high, 1)

            def high_adj(t, b, h):
                act.wait_ge(s_adj_in[b][h], 8 * (t - b) + 16)
                at_least(act, s_half_summed[h], t)
                act.activation(adj_h[h][:, :], adj_raw[b][h][:, :], ACT.Copy).then_inc(s_adj_high, 1)

            act.wait_ge(s_eps, 1)
            act.activation(small[:, 12:13], eps, ACT.Sqrt)
            for t in range(-3, TILES):
                support(t)
                if t + 3 in SPLIT_AT:
                    high_adj(0, 0, SPLIT_AT.index(t + 3))

            def std(t):
                act.wait_ge(s_mean_var2, t + 1)
                act.activation(sd2, mv2[:, 1:2], ACT.Sqrt, bias=eps).then_inc(s_deviation2, 1)

            def neighbours(t, b, more=True):
                high_adj(t, b, 1)
                std(t - 1)
                if more:
                    high_adj(t + 1, 1 - b, 0)

            high_adj(1, 1, 0)
            neighbours(1, 1)
            with act.Fori(1, TILES // 2 - 1) as pair:
                neighbours(2 * pair, 0)
                neighbours(2 * pair + 1, 1)
            neighbours(TILES - 2, 0)
            neighbours(TILES - 1, 1, more=False)

            def high_x(q, b, n=CHUNK):
                act.wait_ge(s_chunk_turned, q + 1)
                at_least(act, s_chunk_up, (q - 1) * HC)
                at_least(act, s_chunk_low, (q - 1) * DC)
                for c in range(DC):
                    act.activation(xTc_h[b][:, c * WIDE:c * WIDE + n * P], bank[6 + c][:, 0:n * P], ACT.Copy
                        ).then_inc(s_chunk_high, 1)

            act.wait_ge(s_half_summed[0], TILES)
            high_x(0, 0)
            std(TILES - 1)

            def exp_of_logits():
                act.wait_ge(s_logit_less_max, 1)
                act.activation(tmp2[:, :], tmp1[:, :], ACT.Exp).then_inc(s_exp, 1)
                act.activation(small[:, 12:13], eps, ACT.Silu)

            def chunk(q, parity, half, n, n_next):
                for m in range(HC):
                    i, b = q * HC + m, m % 2
                    act.wait_ge(s_chunk_up, i + 1)
                    at_least(act, s_chunk_product, i - 1)
                    act.activation(sil[b][:, 0:n * P], bank[2 * b][:, 0:n * P], ACT.Silu).then_inc(s_chunk_silu, 1)
                    act.wait_ge(s_chunk_product, i + 1)
                    at_least(act, s_chunk_down, i - 1)
                    at_least(act, s_chunk_product_low, i - 1)
                    act.activation(gT_h[b][:, 0:n * P], g[b][:, 0:n * P], ACT.Copy).then_inc(s_chunk_product_high, 1)
                    if m == TURN and n_next:
                        high_x(q + 1, 1 - parity, n_next)
                    elif m == TURN:
                        high_xT(0)
                    if isinstance(q, int) and q == CHUNKS and m == 2:
                        exp_of_logits()

            def high_gT(u, h):
                act.wait_ge(s_product_turned[h], u + 1)
                act.activation(gT_h[h][:, 0:HALF], bank[4 + h][:, 0:HALF], ACT.Copy).then_inc(s_product_high[h], 1)

            def high_xT(u):
                act.wait_ge(s_unit_turned, u + 1)
                at_least(act, s_up[1], u)
                act.activation(xT_h[:, :], bank[6][:, 0:D], ACT.Copy).then_inc(s_unit_high, 1)

            def silu(u, h):
                act.wait_ge(s_up[h], u + 1)
                at_least(act, s_product[h], u)
                act.activation(sil[h][:, 0:HALF], bank[2 * h][:, 0:HALF], ACT.Silu).then_inc(s_silu[h], 1)

            def unit(u, last=False):
                first = isinstance(u, int) and u == 0
                if not first:
                    high_gT(u - 1, 0)
                silu(u, 0)
                if not first:
                    high_gT(u - 1, 1)
                if not last:
                    high_xT(u + 1)
                silu(u, 1)

            in_chunks(act.Fori, chunk)
            unit(0)
            with act.Fori(1, SURE) as u:
                unit(u)
            more = units_more(act)
            with act.Fori(SURE, SLOTS - 1) as u:
                with act.If(more + SURE > u):
                    unit(u)
            with act.If(more + SURE > SLOTS - 1):
                unit(SLOTS - 1, last=True)
            high_gT(more + (SURE - 1), 0)
            high_gT(more + (SURE - 1), 1)

        @block.vector
        def _(dve):
            dve.memset(eps, EPS).then_inc(s_eps, 1)
            dve.wait_ge(s_w_gnn_in, 16)
            dve.tensor_copy(w_gnn_h[:, :], w_gnn_raw[:, :]).then_inc(s_w_gnn_split, 1)
            dve.wait_ge(s_w_gnn_split, 1)
            dve.tensor_tensor(w_gnn_l[:, :], w_gnn_raw[:, :], w_gnn_h[:, :].bitcast(F32), ALU.subtract
                ).then_inc(s_w_gnn_split, 1)

            def low_adj(t, b, h):
                dve.wait_ge(s_adj_high, 2 * t + h + 1)
                dve.tensor_tensor(adj_l[b][h][:, :], adj_raw[b][h][:, :], adj_h[h][:, :].bitcast(F32),
                                  ALU.subtract).then_inc(s_adj_low, 1)

            def support(t):
                if t + 4 < TILES:
                    if t + 4 in X_PIECES:
                        dve.wait_ge(s_x_in[X_PIECES.index(t + 4)], 16)
                    at_least(dve, s_mean_var, t + 3)
                    dve.bn_stats(st[t % 2], xtile(t + 4)).then_inc(s_bn_stats, 1)
                if t >= 2:
                    dve.wait_ge(s_support_high, t - 1)
                    dve.scalar_tensor_tensor(out=s_hl[:, (t - 2) * (2 * D) + D:(t - 1) * (2 * D)], in0=bank[2 + t % 2][:, 0:D],
                                             scalar=rs_all[:, t - 2:t - 1],
                                             in1=s_hl[:, (t - 2) * (2 * D):(t - 2) * (2 * D) + D].bitcast(F32),
                                             op0=ALU.mult, op1=ALU.subtract).then_inc(s_support_low, 1)
                if -2 <= t < TILES - 2:
                    dve.wait_ge(s_deviation, t + 3)
                    dve.reciprocal(rs_all[:, t + 2:t + 3], sd_all[:, t + 2:t + 3]).then_inc(s_inverse, 1)
                if 0 <= t < TILES:
                    at_least(dve, s_support, t - 1)
                    dve.wait_ge(s_centred_high, t + 1)
                    dve.tensor_tensor(xcT_l[t % 2][:, :], bank[t % 2][:, 0:D], xcT_h[t % 2][:, :].bitcast(F32),
                                      ALU.subtract).then_inc(s_centred_low, 1)
                if t + 4 < TILES:
                    dve.wait_ge(s_bn_stats, t + 5)
                    dve.bn_aggr(mv_all[:, 2 * (t + 4):2 * (t + 5)], st[t % 2]).then_inc(s_mean_var, 1)

            for t in range(-4, TILES + 2):
                support(t)
                if t + 1 in SPLIT_AT:
                    low_adj(0, 0, SPLIT_AT.index(t + 1))

            def low_xT(u):
                own_wait(dve, s_unit_high, u + 1)
                dve.tensor_copy(meta_id[:, bass.ds(u % RING, 1)], xt[:, ID_COL:ID_COL + 1].bitcast(I32))
                dve.tensor_copy(meta_w[:, bass.ds(u % RING, 1)], xt[:, W_COL:W_COL + 1]).then_inc(s_meta, 1)
                dve.tensor_tensor(xT_l[:, :], bank[6][:, 0:D], xT_h[:, :].bitcast(F32), ALU.subtract).then_inc(s_unit_low, 1)

            def residual(t, acc):
                dve.wait_ge(s_row_block_summed, t + 1)
                dve.wait_ge(s_x_biased, t + 1)
                dve.tensor_tensor(xtile(t), acc[:, 0:D], xtile(t), ALU.add).then_inc(s_x1_part, 1)
                dve.wait_ge(s_x1_part, t + 1)
                dve.tensor_tensor(xtile(t), acc[:, D:2 * D], xtile(t), ALU.add).then_inc(s_x1, 1)
                at_least(dve, s_mean_var2, t)
                own_wait(dve, s_x1, t + 1)
                dve.bn_stats(st2, xtile(t)).then_inc(s_bn_stats2, 1)

            def norm_mean(t):
                at_least(dve, s_x1_normed, t)
                own_wait(dve, s_bn_stats2, t + 1)
                dve.bn_aggr(mv2, st2).then_inc(s_mean_var2, 1)

            def norm(t):
                dve.wait_ge(s_deviation2, t + 1)
                dve.reciprocal(rs2, sd2).then_inc(s_inverse2, 1)
                dve.wait_ge(s_inverse2, t + 1)
                if isinstance(t, int) and t == 0:
                    dve.wait_ge(s_rows_zero, 1)
                dve.tensor_scalar(xn2_all[:, bass.ds(t * ROW, D)], xtile(t), mv2[:, 0:1], rs2,
                                  ALU.subtract, ALU.mult).then_inc(s_x1_normed, 1)

            def row_block(t, b, acc_before):
                residual(t - 1, acc_before)
                norm_mean(t - 1)
                low_adj(t, b, 1)
                norm(t - 1)
                if not isinstance(t, int) or t + 1 < TILES:
                    low_adj(t + 1, 1 - b, 0)

            low_adj(1, 1, 0)
            row_block(1, 1, bank[4])
            with dve.Fori(1, TILES // 2 - 1) as pair:
                row_block(2 * pair, 0, bank[5])
                row_block(2 * pair + 1, 1, bank[4])
            row_block(TILES - 2, 0, bank[5])
            row_block(TILES - 1, 1, bank[4])
            def low_x(q, b, n=CHUNK):
                for c in range(DC):
                    dve.wait_ge(s_chunk_high, q * DC + c + 1)
                    at_least(dve, s_chunk_up, (q - 1) * HC)
                    dve.tensor_tensor(xTc_l[b][:, c * WIDE:c * WIDE + n * P], bank[6 + c][:, 0:n * P],
                                      xTc_h[b][:, c * WIDE:c * WIDE + n * P].bitcast(F32), ALU.subtract
                                          ).then_inc(s_chunk_low, 1)

            low_x(0, 0)
            residual(TILES - 1, bank[5])
            norm_mean(TILES - 1)
            norm(TILES - 1)

            def low_gT(u, h):
                dve.wait_ge(s_product_high[h], u + 1)
                dve.tensor_tensor(gT_l[h][:, 0:HALF], bank[4 + h][:, 0:HALF], gT_h[h][:, 0:HALF].bitcast(F32), ALU.subtract
                    ).then_inc(s_product_low[h], 1)

            def product(u, h):
                dve.wait_ge(s_silu[h], u + 1)
                at_least(dve, s_product_turned[h], u)
                dve.tensor_tensor(g[h][:, 0:HALF], bank[2 * h + 1][:, 0:HALF], sil[h][:, 0:HALF], ALU.mult
                    ).then_inc(s_product[h], 1)

            def routed_y(u):
                r = u % RING
                at_least(dve, s_added, 16 * u - 16 * (RING - 1))
                dve.wait_ge(s_meta, u + 1)
                own_wait(dve, s_down, u + 1)
                dve.tensor_copy(id_ring[:, bass.ds(r, 1)], meta_id[:, bass.ds(u % RING, 1)])
                dve.tensor_scalar(y_ring[:, bass.ds(r * D, D)], bank[7][:, 0:D], meta_w[:, bass.ds(u % RING, 1)],
                                  None, ALU.mult).then_inc(s_y_taken, 1)

            def tile8(buf, t, n=1):
                return buf[:, bass.ds(t * E, n * E)]

            def e_last(ap):
                return ap.rearrange("p (t e) -> p t e", e=E)

            def router(q, n, m):
                t = q * CHUNK
                if m == 1:
                    dve.wait_ge(s_logit_parts, q + 1)
                    pair = bank[6][:, 0:n * 2 * E].rearrange("p (t e) -> p t e", e=2 * E)
                    dve.tensor_copy(e_last(logit_l[:, 0:n * E]), pair[:, :, E:]).then_inc(s_logit_low, 1)
                    dve.wait_ge(s_logit_low, q + 1)
                    dve.tensor_tensor(e_last(logit[:, 0:n * E]), pair[:, :, 0:E], e_last(logit_l[:, 0:n * E]),
                                      ALU.add).then_inc(s_logit, 1)
                if m == 2:
                    own_wait(dve, s_logit, q + 1)
                    for j in range(n):
                        dve.max(m8[:, j * E:(j + 1) * E], logit[:, j * E:(j + 1) * E]).then_inc(s_best8, 1)
                    own_wait(dve, s_best8, q * CHUNK + n)
                    for j in range(n):
                        dve.max_index(i8[:, j * E:(j + 1) * E], m8[:, j * E:(j + 1) * E],
                                      logit[:, j * E:(j + 1) * E]).then_inc(s_best8_number, 1)
                if m == 3:
                    own_wait(dve, s_best8_number, q * CHUNK + n)
                    dve.tensor_copy(tile8(m8_all, t, n), m8[:, 0:n * E])
                    dve.tensor_copy(i2f[0][:, 0:n], i8[:, 0:n * E:E])
                    dve.tensor_copy(i2f[1][:, 0:n], i8[:, 1:n * E:E]).then_inc(s_best2_number, 1)
                if m == 4:
                    own_wait(dve, s_best2_number, q + 1)
                    for oh, number in zip((oh1, oh2), i2f):
                        dve.tensor_tensor(e_last(tile8(oh, t, n)), iota8.unsqueeze(1).to_broadcast([P, n, E]),
                                          number[:, 0:n].unsqueeze(2).to_broadcast([P, n, E]), ALU.is_equal
                                              ).then_inc(s_one_hot, 1)
                if m == 5:
                    own_wait(dve, s_one_hot, 2 * q + 2)
                    dve.tensor_tensor(tile8(chosen, t, n), tile8(oh1, t, n), tile8(oh2, t, n), ALU.add).then_inc(s_chosen, 1)
                    dve.wait_ge(s_chosen, q + 1)
                    for j in range(n):
                        dve.wait_ge(s_before, t + j + 1)
                        dve.tensor_tensor(tile8(before, t + j + 1), tile8(before, t + j), tile8(chosen, t + j),
                                          ALU.add).then_inc(s_before, 1)

            def chunk_y(q, t, n):
                dve.wait_ge(s_chunk_down, (q + 1) * HC)
                for k in range(0, n, 2):
                    x1 = x_all[:, bass.ds((t + k) * D, 2 * D)]
                    added = dve.tensor_tensor(x1, bank[4 + k // 2][:, 0:2 * D], x1, ALU.add)
                added.then_inc(s_chunk_added, 1)

            def chunk(q, parity, half, n, n_next):
                peeled = isinstance(q, int)
                for m in range(HC):
                    i, b = q * HC + m, m % 2
                    dve.wait_ge(s_chunk_silu, i + 1)
                    at_least(dve, s_chunk_product_low, i - 1)
                    dve.tensor_tensor(g[b][:, 0:n * P], bank[2 * b + 1][:, 0:n * P], sil[b][:, 0:n * P], ALU.mult
                        ).then_inc(s_chunk_product, 1)
                    if m == 0 and peeled and q > 0:
                        chunk_y(q - 1, (q - 1) % CHUNKS * CHUNK, tiles_in(q - 1))
                    elif m == 0 and not peeled:
                        chunk_y(q - 1, (q - (1 + half * CHUNKS)) * CHUNK, CHUNK)
                    if m == TURN + 1 and n_next:
                        low_x(q + 1, 1 - parity, n_next)
                    elif m == TURN + 1:
                        low_xT(0)
                    if half == 0:
                        router(q, n, m)
                    if peeled and half == 1:
                        routing(q, m)
                    dve.wait_ge(s_chunk_product_high, i + 1)
                    at_least(dve, s_chunk_down, i - 1)
                    dve.tensor_tensor(gT_l[b][:, 0:n * P], g[b][:, 0:n * P], gT_h[b][:, 0:n * P].bitcast(F32),
                                      ALU.subtract).then_inc(s_chunk_product_low, 1)

            def unit(u, last=False):
                first = isinstance(u, int) and u == 0
                if not first:
                    low_gT(u - 1, 0)
                if not isinstance(u, int) or u >= 2:
                    routed_y(u - 2)
                product(u, 0)
                if first:
                    chunk_y(2 * CHUNKS - 1, LAST * CHUNK, tiles_in(LAST))
                else:
                    low_gT(u - 1, 1)
                if not last:
                    low_xT(u + 1)
                product(u, 1)

            chain = [0]

            def step(ins):
                chain[0] += 1
                ins.then_inc(s_routing_step, 1)
                dve.wait_ge(s_routing_step, chain[0])

            def by_tile(buf):
                return buf[:, :].rearrange("p (t e) -> p t e", e=E)

            def over_tiles(buf, n=TILES, parts=P):
                return buf.unsqueeze(1).to_broadcast([parts, n, E])

            def route_1():
                dve.wait_ge(s_ranks, 1)
                dve.tensor_copy(pos_e[:, :], bank[6][:, 0:TILES * E])
                dve.tensor_scalar(n_i[:, :], bank[6][:, TILES * E:(TILES + 1) * E], float(P - 1), None,
                                  ALU.add).then_inc(s_ranks_read, 1)
                dve.wait_ge(s_ranks_read, 1)
                step(dve.tensor_scalar(n_t[:, :], n_i[:, :], 7, None, ALU.arith_shift_right))
                step(dve.tensor_copy(tiles_f[:, :], n_t[:, :]))
                step(dve.tensor_tensor_scan(end_f[:, :], ones8[:, :], tiles_f[:, :], 0.0, ALU.mult, ALU.add))
                step(dve.tensor_tensor(start_f[:, :], end_f[:, :], tiles_f[:, :], ALU.subtract))

            def route_2():
                dve.wait_ge(s_exp, 1)
                step(dve.scalar_tensor_tensor(out=by_tile(pos_e), in0=over_tiles(start_f[:, :]), scalar=float(P),
                                              in1=by_tile(pos_e), op0=ALU.mult, op1=ALU.add))
                for oh, pos_f, pos in ((oh1, pos1f, pos1), (oh2, pos2f, pos2)):
                    step(dve.tensor_tensor(tmp1[:, :], oh[:, :], pos_e[:, :], ALU.mult))
                    step(dve.tensor_reduce(pos_f[:, :], by_tile(tmp1), AX_X, ALU.add))
                    dve.tensor_copy(pos[:, :], pos_f[:, :]).then_inc(s_places, 1)
                step(dve.memset(ones_s[:, :], 1.0))

            def route_0():
                dve.wait_ge(s_before, TILES + 1)
                dve.tensor_tensor(by_tile(tmp1), by_tile(m8_all),
                                  m8_all[:, 0::E].unsqueeze(2).to_broadcast([P, TILES, E]), ALU.subtract
                                      ).then_inc(s_logit_less_max, 1)

            def route_3():
                step(dve.tensor_reduce(esum[:, :], by_tile(tmp2), AX_X, ALU.add))
                step(dve.reciprocal(esum[:, :], esum[:, :]))
                step(dve.tensor_tensor(w2[:, :], esum[:, :], tmp2[:, 1::E], ALU.mult))
                dve.tensor_tensor(xn2_all[:, W_COL::ROW], esum[:, :], tmp2[:, 0::E], ALU.mult).then_inc(s_weight1, 1)

            def route_4():
                iota_s = consts[0:1, IOTA_S:IOTA_S + SLOTS].unsqueeze(2).to_broadcast([1, SLOTS, E])
                ends = over_tiles(end_f[0:1, :], SLOTS, 1)
                a8 = slot8a[:, :].rearrange("p (s e) -> p s e", e=E)
                step(dve.tensor_tensor(a8, ends, iota_s, ALU.is_le))
                step(dve.tensor_reduce(e_of[:, 1:], a8, AX_X, ALU.add))
                step(dve.tensor_scalar(e_of[:, 1:], e_of[:, 1:], float(E - 1), None, ALU.min))
                dve.tensor_scalar(more_i[:, :], end_f[0:1, E - 1:E], float(-SURE), None, ALU.add)
                dve.tensor_copy(e0_i[:, :], e_of[:, 1:2]).then_inc(s_first_expert, 1)

            def route_5():
                ends = over_tiles(end_f[0:1, :], SLOTS, 1)
                a8, b8 = e_last(slot8a[:, :]), e_last(slot8b[:, :])
                step(dve.scalar_tensor_tensor(out=b8, in0=a8, scalar=1024.0, in1=ends, op0=ALU.mult, op1=ALU.add))
                step(dve.tensor_reduce(end_of[:, :], b8, AX_X, ALU.min))

            def route_6():
                ends = over_tiles(end_f[0:1, :], SLOTS, 1)
                a8 = slot8a[:, :].rearrange("p (s e) -> p s e", e=E)
                step(dve.tensor_tensor(a8, ends, end_of[:, :].unsqueeze(2).to_broadcast([1, SLOTS, E]), ALU.is_le))
                step(dve.tensor_reduce(next_of[:, :], a8, AX_X, ALU.add))
                step(dve.tensor_scalar(next_i[:, :], next_of[:, :], float(E - 1), None, ALU.min))

            def route_7():
                step(dve.tensor_tensor(first_of[:, :], e_of[:, 1:], e_of[:, 0:SLOTS], ALU.not_equal))
                step(dve.tensor_tensor_scan(run_of[:, 1:], ones_s[:, :], first_of[:, :], 0.0, ALU.mult, ALU.add))

            def route_8():
                step(dve.tensor_copy(run_i[:, :], run_of[:, :]))
                step(dve.tensor_scalar(par_i[:, :], run_i[:, :], 1, None, ALU.bitwise_and))
                step(dve.tensor_scalar(par_i[:, :], par_i[:, :], -1.0, 1.0, ALU.mult, ALU.add))
                step(dve.scalar_tensor_tensor(out=flag_of[:, :], in0=e_of[:, 1:], scalar=float(E - 1), in1=first_of[:, :],
                                              op0=ALU.is_lt, op1=ALU.mult))
                step(dve.scalar_tensor_tensor(out=runs_i[:, :], in0=run_of[:, 0:SLOTS], scalar=16.0, in1=run_of[:, 1:],
                                              op0=ALU.mult, op1=ALU.add))
                step(dve.tensor_copy(flag_i[:, :], flag_of[:, :]))
                step(dve.tensor_tensor(fetch_i[0][:, :], flag_i[:, :], par_i[:, 1:], ALU.mult))
                dve.tensor_tensor(fetch_i[1][:, :], flag_i[:, :], fetch_i[0][:, :], ALU.subtract).then_inc(s_tables, 1)

            def routing(q, m):
                if q == CHUNKS:
                    if m == 0:
                        route_0()
                    if m == 2:
                        route_1()
                    if m == 3:
                        route_2()
                    if m == 4:
                        route_3()
                    if m == 5:
                        route_4()
                if q == 2 * CHUNKS - 2:
                    if m == 1:
                        route_5()
                    if m == 2:
                        route_6()
                    if m == 3:
                        route_7()
                    if m == 4:
                        route_8()

            dve.wait_ge(s_row_block_summed, TILES)
            dve.memset(tile8(before, 0), 0.0).then_inc(s_before, 1)
            dve.memset(ones8[:, :], 1.0)
            dve.memset(e_of[:, 0:1], -1.0)
            dve.memset(run_of[:, 0:1], 0.0)
            dve.wait_ge(s_weights_low, 1)
            for c in range(DC):
                for low in range(2):
                    at = low * WCOLS + c * W1_COLS + HID
                    dve.tensor_copy(gate_hl[:, (2 * c + low) * E:(2 * c + low + 1) * E], W[:, at:at + E].bitcast(F32)
                        ).then_inc(s_gate, 1)

            in_chunks(dve.Fori, chunk)
            dve.wait_ge(s_chunk_product_low, 2 * CHUNKS * HC)
            for u in range(RING + 2):
                unit(u)
            with dve.Fori(RING + 2, SURE) as u:
                unit(u)
            more = units_more(dve)
            with dve.Fori(SURE, SLOTS - 1) as u:
                with dve.If(more + SURE > u):
                    unit(u)
            with dve.If(more + SURE > SLOTS - 1):
                unit(SLOTS - 1, last=True)
            low_gT(more + (SURE - 1), 0)
            routed_y(more + (SURE - 2))
            low_gT(more + (SURE - 1), 1)
            routed_y(more + (SURE - 1))

        @block.tensor
        def _(pe):
            def transposes(dst, src, n):
                for c in range(n):
                    mm = pe.transpose(dst[:, c * P:(c + 1) * P], src[:, c * P:(c + 1) * P], ident)
                return mm

            def turn_x(t):
                pe.wait_ge(s_centred, t + 1)
                at_least(pe, s_centred_low, t - 1)
                transposes(bank[t % 2], xc[t % 2], DC).then_inc(s_centred_turned, 1)

            def support(t):
                pe.wait_ge(s_centred_low, t + 1)
                at_least(pe, s_support_low, t - 1)
                k = 0
                for c in range(DC):
                    high, low = xcT_h[t % 2][:, c * P:(c + 1) * P], xcT_l[t % 2][:, c * P:(c + 1) * P]
                    wh, wl = w_gnn_h[:, c * D:(c + 1) * D], w_gnn_l[:, c * D:(c + 1) * D]
                    for lhs, rhs in ((high, wh), (high, wl), (low, wh)):
                        mm = pe.matmul(bank[2 + t % 2][:, 0:D], lhs, rhs, start=(k == 0), stop=(k == 3 * DC - 1))
                        k += 1
                mm.then_inc(s_support, 1)

            def neighbour(b, j):
                h, k = j // HALF_J, j % HALF_J
                high, low = adj_h[h][:, k * P:(k + 1) * P], adj_l[b][h][:, k * P:(k + 1) * P]
                acc = bank[4 + b]
                pe.matmul(acc[:, 0:2 * D], high, s_hl[:, j * 2 * D:(j + 1) * 2 * D], start=(j == 0), stop=False)
                mm = pe.matmul(acc[:, D:2 * D], low, s_hl[:, j * 2 * D:j * 2 * D + D], start=False, stop=(j == TILES - 1))
                if k == HALF_J - 1:
                    mm.then_inc(s_half_summed[h], 1)

            def row_block(t, b):
                at_least(pe, s_x1, t - 1)
                for j in range(TILES):
                    if j % HALF_J == 0:
                        pe.wait_ge(s_adj_low, 2 * t + j // HALF_J + 1)
                    neighbour(b, j)

            def loop(first, end):
                return nc.Fori(first, end, engines=(mybir.EngineType.PE,), hint_back_edge=True)

            pe.wait_ge(s_consts_in, 16)
            turn_x(0)
            turn_x(1)
            pe.wait_ge(s_w_gnn_split, 2)
            for t in range(TILES + BEHIND):
                if t < TILES:
                    support(t)
                if t + 2 < TILES:
                    turn_x(t + 2)
                j = t - BEHIND
                if j >= 0:
                    if j % HALF_J == 0:
                        pe.wait_ge(s_adj_low, j // HALF_J + 1)
                    pe.wait_ge(s_support_low, j + 1)
                    neighbour(0, j)
            row_block(1, 1)
            with loop(1, TILES // 2 - 1) as pair:
                row_block(2 * pair, 0)
                row_block(2 * pair + 1, 1)
            row_block(TILES - 2, 0)
            def turn_rows(q, half, n):
                pe.wait_ge(s_chunk_in, 16 * q + 16)
                at_least(pe, s_chunk_low, q * DC)
                if half == 0:
                    at_least(pe, s_logit, q)
                for c in range(DC):
                    for j in range(n):
                        mm = pe.transpose(bank[6 + c][:, j * P:(j + 1) * P], rows_in[:, j * ROW + c * P:j * ROW + (c + 1) * P], ident)
                mm.then_inc(s_chunk_turned, 1)

            turn_rows(0, 0, CHUNK)
            row_block(TILES - 1, 1)

            def chunk_up(q, b, m, buffer, n):
                pe.wait_ge(s_chunk_low, q * DC + DC)
                at_least(pe, s_chunk_product, q * HC + m - 1)
                for part, dst in ((0, bank[m % 2 * 2]), (1, bank[m % 2 * 2 + 1])):
                    k = 0
                    for c in range(DC):
                        x_h, x_l = (x[b][:, c * WIDE:c * WIDE + n * P] for x in (xTc_h, xTc_l))
                        at = buffer * 2 * WCOLS + PART_AT[part] + c * (PARTS[part] // DC) + m * P
                        w_h, w_l = W[:, at:at + P], W[:, at + WCOLS:at + WCOLS + P]
                        for w, moving in ((w_h, x_h), (w_h, x_l), (w_l, x_h)):
                            mm = pe.matmul(dst[:, 0:n * P], w, moving, start=(k == 0), stop=(k == 3 * DC - 1))
                            k += 1
                mm.then_inc(s_chunk_up, 1)

            def chunk_down(q, m, buffer, n):
                i = q * HC + m
                pe.wait_ge(s_chunk_product_low, i + 1)
                if m == 0:
                    at_least(pe, s_chunk_added, q)
                for j in range(n):
                    high, low = (x[m % 2][:, j * P:(j + 1) * P] for x in (gT_h, gT_l))
                    at = buffer * 2 * WCOLS + PART_AT[2] + m * D
                    w_h, w_l = W[:, at:at + D], W[:, at + WCOLS:at + WCOLS + D]
                    for k, (a, w) in enumerate(((high, w_h), (high, w_l), (low, w_h))):
                        mm = pe.matmul(bank[4 + j // 2][:, j % 2 * D:(j % 2 + 1) * D], a, w, start=(m == 0 and k == 0 and j % 2 == 0),
                                       stop=(m == HC - 1 and k == 2), skip_group_check=True)
                mm.then_inc(s_chunk_down, 1)

            def chunk_logits(q, b, n):
                for j in range(n):
                    at = bank[6][:, j * 2 * E:(j + 1) * 2 * E]
                    for c in range(DC):
                        high, low = (x[b][:, c * WIDE + j * P:c * WIDE + (j + 1) * P] for x in (xTc_h, xTc_l))
                        hl = gate_hl[:, c * 2 * E:(c + 1) * 2 * E]
                        pe.matmul(at, high, hl, start=(c == 0), stop=False, skip_group_check=True)
                        mm = pe.matmul(at[:, 0:E], low, hl[:, 0:E], start=False, stop=(c == DC - 1), skip_group_check=True)
                mm.then_inc(s_logit_parts, 1)

            def chunk(q, parity, half, n, n_next):
                peeled = isinstance(q, int)
                for m in range(1, HC):
                    chunk_up(q, parity, m, half, n)
                    if m == 1 and half == 0:
                        if peeled and q == 0:
                            pe.wait_ge(s_gate, 2 * DC)
                        chunk_logits(q, parity, n)
                    if m == 1 and peeled and q == CHUNKS:
                        ranks()
                    if m == TURN:
                        if peeled and q == CHUNKS:
                            pe.wait_ge(s_ranks_read, 1)
                        if n_next:
                            turn_rows(q + 1, half, n_next)
                        else:
                            xT_of(0)
                    if peeled and m == 1 and q % CHUNKS == 0:
                        pe.wait_ge(s_weights_low, 3 * half + 3)
                    chunk_down(q, m - 1, half, n)
                if n_next:
                    half_next = half
                    if peeled and q == CHUNKS - 1:
                        half_next = 1
                        pe.wait_ge(s_weights_low, 5)
                    chunk_up(q + 1, 1 - parity, 0, half_next, n_next)
                    chunk_down(q, HC - 1, half, n)

            def w_part(buffer, low, part):
                def at(col, n):
                    return W[:, bass.ds(buffer * (2 * WCOLS) + (low * WCOLS + PART_AT[part] + col), n)]
                return at

            def xT_of(u):
                pe.wait_ge(s_unit_in, 16 * u + 16)
                at_least(pe, s_unit_low, u)
                transposes(bank[6], xt, DC).then_inc(s_unit_turned, 1)

            def up(u, h, buffer):
                pe.wait_ge(s_unit_low, u + 1)
                if isinstance(u, int) and u == 0:
                    pe.wait_ge(s_chunk_product, 2 * CHUNKS * HC - 1 + h)
                at_least(pe, s_product[h], u)
                for part, dst in ((0, bank[2 * h]), (1, bank[2 * h + 1])):
                    k = 0
                    for c in range(DC):
                        high, low = xT_h[:, c * P:(c + 1) * P], xT_l[:, c * P:(c + 1) * P]
                        col = c * (PARTS[part] // DC) + h * HALF
                        for a, b in ((high, 0), (high, 1), (low, 0)):
                            mm = pe.matmul(dst[:, 0:HALF], a, w_part(buffer, b, part)(col, HALF), start=(k == 0),
                                           stop=(k == 3 * DC - 1))
                            k += 1
                mm.then_inc(s_up[h], 1)

            def turn(u, h):
                pe.wait_ge(s_product[h], u + 1)
                at_least(pe, s_product_low[h], u)
                if isinstance(u, int) and u == 0:
                    pe.wait_ge(s_chunk_added, 2 * CHUNKS)
                transposes(bank[4 + h], g[h], HC // 2).then_inc(s_product_turned[h], 1)

            def down(u, h, buffer):
                pe.wait_ge(s_product_low[h], u + 1)
                if h == 0:
                    at_least(pe, s_y_taken, u)
                for k in range(HC // 2):
                    high, low = gT_h[h][:, k * P:(k + 1) * P], gT_l[h][:, k * P:(k + 1) * P]
                    col = (h * (HC // 2) + k) * D
                    for n, (a, b) in enumerate(((high, 0), (high, 1), (low, 0))):
                        mm = pe.matmul(bank[7][:, 0:D], a, w_part(buffer, b, 2)(col, D), start=(h == 0 and k == 0 and n == 0),
                                       stop=(h == 1 and k == HC // 2 - 1 and n == 2))
                if h == 1:
                    mm.then_inc(s_down, 1)

            def ranks():
                pe.wait_ge(s_before, TILES + 1)
                pe.matmul(bank[6][:, 0:TILES * E], tri, chosen[:, :], start=True, stop=False, skip_group_check=True)
                pe.matmul(bank[6][:, 0:TILES * E], ones_pp, before[:, 0:TILES * E], start=False, stop=True, skip_group_check=True)
                pe.matmul(bank[6][:, TILES * E:(TILES + 1) * E], ones_pp, before[:, TILES * E:(TILES + 1) * E], start=False,
                          stop=True, skip_group_check=True).then_inc(s_ranks, 1)

            def unit(u, buffer, buffer_before, whole, whole_before, last=False):
                first = isinstance(u, int) and u == 0
                pe.wait_ge(s_weights_low, whole - 1)
                up(u, 0, buffer)
                if first:
                    chunk_down(2 * CHUNKS - 1, HC - 1, 1, tiles_in(LAST))
                else:
                    turn(u - 1, 1)
                if not last:
                    xT_of(u + 1)
                up(u, 1, buffer)
                if not first:
                    pe.wait_ge(s_weights_low, whole_before)
                    down(u - 1, 0, buffer_before)
                turn(u, 0)
                if not first:
                    down(u - 1, 1, buffer_before)

            pe.wait_ge(s_weights_low, 2)
            chunk_up(0, 0, 0, 0, CHUNK)
            in_chunks(loop, chunk)
            more = units_more(pe)

            def routed(s, last=False):
                both = pe.value_load(runs_i[0:1, bass.ds(s, 1)], min_val=1, max_val=16 * E + E)
                run, run_before = both % 16, both // 16
                par, par_before = (run + 1) % 2, (run_before + 1) % 2
                unit(s, par, par_before, whole=run * 3 + 6, whole_before=run_before * 3 + 6, last=last)

            routed(0)
            with loop(1, SURE) as s:
                routed(s)
            with loop(SURE, SLOTS - 1) as s:
                with pe.If(more + SURE > s):
                    routed(s)
            with pe.If(more + SURE > SLOTS - 1):
                routed(SLOTS - 1, last=True)
            run = pe.value_load(run_i[0:1, bass.ds(more + SURE, 1)], min_val=1, max_val=E)
            par = (run + 1) % 2
            pe.wait_ge(s_weights_low, run * 3 + 6)
            turn(more + (SURE - 1), 1)
            down(more + (SURE - 1), 0, par)
            down(more + (SURE - 1), 1, par)


def kernel(x, adj, L0_gnn_weight, L0_gnn_bias, L0_ffn_gate_w, L0_ffn_w1, L0_ffn_w3, L0_ffn_w2,
           L0_ffn_sw1, L0_ffn_sw3, L0_ffn_sw2):
    import concourse.bacc as bacc
    from concourse.bass_utils import run_bass_kernel_spmd

    def np32(a):
        return np.asarray(a, dtype=np.float32)

    def features_on_partitions(w):
        return np.ascontiguousarray(w.T.reshape(DC, P, -1).transpose(1, 0, 2)).reshape(P, -1)

    x, adj = np32(x), np32(adj)
    pad = NP - N
    x_in = np.pad(x, ((0, pad), (0, 0))).reshape(TILES, P, D).transpose(1, 0, 2).reshape(P, TILES * D)
    adj_p = np.pad(adj, ((0, pad), (0, pad))).reshape(TILES, P, TILES, P)
    adj_in = np.ascontiguousarray(adj_p.transpose(0, 3, 2, 1)).reshape(TILES * P, TILES * P)
    w_in = np32(L0_gnn_weight).reshape(DC, P, D).transpose(1, 0, 2).reshape(P, DC * D)
    bias_in = np.tile(np32(L0_gnn_bias)[None, :], (P, 1))
    gate = np32(L0_ffn_gate_w)
    sw1, sw3, sw2 = np32(L0_ffn_sw1), np32(L0_ffn_sw3), np32(L0_ffn_sw2)
    w1 = list(sw1.reshape(2, HID, D)) + list(np32(L0_ffn_w1))
    w3 = list(sw3.reshape(2, HID, D)) + list(np32(L0_ffn_w3))
    w2 = [sw2[:, :HID], sw2[:, HID:]] + list(np32(L0_ffn_w2))
    down = [np.ascontiguousarray(w.T.reshape(HC, P, D).transpose(1, 0, 2)).reshape(P, -1) for w in w2]
    w1 = [np.concatenate([w, gate if n == 0 else np.zeros_like(gate)]) for n, w in enumerate(w1)]
    experts_in = np.concatenate([np.concatenate([features_on_partitions(a), features_on_partitions(b), c], axis=1)
                                 for a, b, c in zip(w1, w3, down)])
    cst = np.zeros((P, CST), np.float32)
    cst[:, IDENT:IDENT + P] = np.eye(P)
    cst[:, TRI:TRI + P] = np.triu(np.ones((P, P)), 1)
    cst[:, IOTA8:IOTA8 + E] = np.arange(E)
    cst[:, ONES:ONES + P] = 1
    cst[:, IOTA_S:IOTA_S + SLOTS] = np.arange(SLOTS)

    nc = bacc.Bacc("TRN2", target_bir_lowering=False, num_devices=1)
    arrays = {"x_in": x_in, "adj_in": adj_in, "w_in": w_in, "bias_in": bias_in,
              "experts_in": experts_in, "cst_in": cst}
    arrays = {k: np.ascontiguousarray(v) for k, v in arrays.items()}
    args = [nc.dram_tensor(k, list(v.shape), F32, kind="ExternalInput").ap() for k, v in arrays.items()]
    out = nc.dram_tensor("out", [NP + P, D], F32, kind="ExternalOutput").ap()
    build(nc, *args, out)
    r = run_bass_kernel_spmd(nc, [arrays], core_ids=[0])
    return r.results[0]["out"][:N]
```
